# Optimizing a Trainium2 kernel written in Bass

```python
import numpy as np
import jax
import jax.numpy as jnp

def _softmax(x, axis=-1):
    return jax.nn.softmax(x, axis=axis)

def _gelu(x):
    return jax.nn.gelu(x, approximate=True)

def _silu(x):
    return jax.nn.silu(x)

def _sigmoid(x):
    return jax.nn.sigmoid(x)

def _layernorm(x, axis=-1, eps=1e-05):
    m = jnp.mean(x, axis=axis, keepdims=True)
    v = jnp.var(x, axis=axis, keepdims=True)
    return (x - m) / jnp.sqrt(v + eps)

def _scatter_add(tgt, idx, src, axis=0):
    return tgt.at[idx].add(src)

def _segment_sum(src, seg, n):
    return jax.ops.segment_sum(src, seg, n)
kernel_name = 'mk_xattn_ffn_d1_seqx_r2_7e6635'

def setup_inputs(seed: int=0):
    np.random.seed(seed)
    _w = jnp.asarray

    def _rec_inputs():
        import jax
        import jax.numpy as jnp
        _rk = jax.random.key(seed)
        x = -0.0005207 + 1.001 * jax.random.normal(jax.random.fold_in(_rk, 1), (8, 512, 512), jnp.float32)
        _lenS = 512 - jax.random.randint(jax.random.fold_in(_rk, 7), (8,), 0, max(1, 512 // 4) + 1, jnp.int32)
        _lenS2 = 77 - jax.random.randint(jax.random.fold_in(_rk, 8), (8,), 0, max(1, 77 // 4) + 1, jnp.int32)
        _ctx_1024P = jax.random.normal(jax.random.fold_in(_rk, 12), (8, 16, 512), jnp.float32)
        _ctx_1024c = jax.random.dirichlet(jax.random.fold_in(_rk, 512), 0.3 * jnp.ones((16,), jnp.float32), (8, 77))
        _ctx_1024t = jnp.einsum('bsk,bkd->bsd', _ctx_1024c, _ctx_1024P)
        _ctx_1024t = _ctx_1024t * jax.lax.rsqrt(jnp.mean(jnp.square(_ctx_1024t)) + 1e-12) * 0.953939
        ctx_1024 = 0.00191187 + 0.999416 * (_ctx_1024t + 0.3 * jax.random.normal(jax.random.fold_in(_rk, 612), (8, 77, 512), jnp.float32))
        _validS = jnp.arange(512)[None, :] < _lenS[:, None]
        _validS2 = jnp.arange(77)[None, :] < _lenS2[:, None]
        _causal = jnp.tril(jnp.ones((512, 512), dtype=bool))
        mask_BxS_ff1 = jnp.where(jnp.ones((8, 512), dtype=bool), 1.0, 0.0).astype(jnp.float32)
        mask_BxS2_ik0 = jnp.where(jnp.broadcast_to(_validS2[:, :], (8, 77)), 0, 1).astype(jnp.int32)
        return (x, ctx_1024, mask_BxS_ff1, mask_BxS2_ik0)
    x, ctx_1024, mask_BxS_ff1, mask_BxS2_ik0 = _rec_inputs()

    def _L0_xattn_setup():
        import jax, jax.numpy as jnp
        import numpy as np
        B, F, T, D = (8, 128, 32, 512)
        NEG = -1e+30
        key = jax.random.key(seed)
        ks = jax.random.split(key, 10)
        s = 1.0 / np.sqrt(D)
        return {'features': jax.random.normal(ks[0], (B, F, D), jnp.float32), 'masks': jnp.ones((B, F), jnp.float32), 'textual_features': jax.random.normal(ks[1], (B, T, D), jnp.float32), 'q_masks': jax.random.randint(ks[2], (B, T), 0, 2, jnp.int32), 'Ws': jax.random.normal(ks[3], (D, D), jnp.float32) * s, 'W': jax.random.normal(ks[4], (D, D), jnp.float32) * s, 'w': jax.random.normal(ks[5], (D, 1), jnp.float32) * s, 'b': jax.random.normal(ks[6], (1, D), jnp.float32) * s, 'Wcw': jax.random.normal(ks[7], (1, D), jnp.float32) * s, 'bcw': jnp.zeros((1,), jnp.float32), 'Wcb': jax.random.normal(ks[8], (1, D), jnp.float32) * s, 'bcb': jnp.zeros((1,), jnp.float32)}
    _L0_xattn_all = _L0_xattn_setup()
    _L0_xattn_in = {k: v for k, v in _L0_xattn_all.items() if k in ('Ws', 'W', 'w', 'b', 'Wcw', 'bcw', 'Wcb', 'bcb')}
    del _L0_xattn_all

    def _L0_ffn_setup():
        import math
        import jax, jax.numpy as jnp
        import numpy as np
        B, L, D, F_FF, E = (4, 1024, 512, 2048, 8)
        TOP_K = 1
        CAPACITY_FACTOR = 1.25
        key = jax.random.key(seed)
        ks = jax.random.split(key, 4)
        h = jax.random.normal(ks[0], (B, L, D), dtype=jnp.float32)
        gate_w = jax.random.normal(ks[1], (E, D), dtype=jnp.float32) * 0.02
        gate_b = jnp.zeros((E,), dtype=jnp.float32)
        w1 = jax.random.normal(ks[2], (E, D, F_FF), dtype=jnp.float32) * 0.02
        b1 = jnp.zeros((E, F_FF), dtype=jnp.float32)
        w2 = jax.random.normal(ks[3], (E, F_FF, D), dtype=jnp.float32) * 0.02
        b2 = jnp.zeros((E, D), dtype=jnp.float32)
        return {'h': h, 'gate_w': gate_w, 'gate_b': gate_b, 'w1': w1, 'b1': b1, 'w2': w2, 'b2': b2}
    _L0_ffn_all = _L0_ffn_setup()
    _L0_ffn_in = {k: v for k, v in _L0_ffn_all.items() if k in ('gate_w', 'gate_b', 'w1', 'b1', 'w2', 'b2')}
    del _L0_ffn_all
    return {'x': x, 'ctx_1024': ctx_1024, 'mask_BxS_ff1': mask_BxS_ff1, 'mask_BxS2_ik0': mask_BxS2_ik0, 'L0_xattn_Ws': _L0_xattn_in['Ws'], 'L0_xattn_W': _L0_xattn_in['W'], 'L0_xattn_w': _L0_xattn_in['w'], 'L0_xattn_b': _L0_xattn_in['b'], 'L0_xattn_Wcw': _L0_xattn_in['Wcw'], 'L0_xattn_bcw': _L0_xattn_in['bcw'], 'L0_xattn_Wcb': _L0_xattn_in['Wcb'], 'L0_xattn_bcb': _L0_xattn_in['bcb'], 'L0_ffn_gate_w': _L0_ffn_in['gate_w'], 'L0_ffn_gate_b': _L0_ffn_in['gate_b'], 'L0_ffn_w1': _L0_ffn_in['w1'], 'L0_ffn_b1': _L0_ffn_in['b1'], 'L0_ffn_w2': _L0_ffn_in['w2'], 'L0_ffn_b2': _L0_ffn_in['b2']}

def reference(x, ctx_1024, mask_BxS_ff1, mask_BxS2_ik0, L0_xattn_Ws, L0_xattn_W, L0_xattn_w, L0_xattn_b, L0_xattn_Wcw, L0_xattn_bcw, L0_xattn_Wcb, L0_xattn_bcb, L0_ffn_gate_w, L0_ffn_gate_b, L0_ffn_w1, L0_ffn_b1, L0_ffn_w2, L0_ffn_b2):
    import jax
    import jax.numpy as jnp

    def _L0_xattn_ref(features, masks, textual_features, q_masks, Ws, W, w, b, Wcw, bcw, Wcb, bcb):
        import jax, jax.numpy as jnp
        import numpy as np
        B, F, T, D = (8, 128, 32, 512)
        NEG = -1e+30
        txt_proj = jnp.einsum('btd,de->bte', textual_features, Ws)
        feat_proj = jnp.einsum('bfd,de->bfe', features, W)
        h = jnp.tanh(txt_proj[:, None, :, :] + feat_proj[:, :, None, :] + b[None, None, :, :][..., 0, :])
        rho = jnp.einsum('bftd,d->bft', h, w[:, 0])
        qm = q_masks.astype(jnp.float32)
        rho = rho + (1.0 - qm)[:, None, :] * NEG
        att = jax.nn.softmax(rho, axis=-1)
        txt_h = jnp.einsum('bft,btd->bfd', att, textual_features)
        w_s = jnp.tanh(jnp.einsum('bfd,od->bfo', txt_h, Wcw) + bcw)
        b_s = jnp.tanh(jnp.einsum('bfd,od->bfo', txt_h, Wcb) + bcb)
        return w_s * features + b_s

    def _L0_ffn_ref(h, gate_w, gate_b, w1, b1, w2, b2):
        import math
        import jax, jax.numpy as jnp
        import numpy as np
        B, L, D, F_FF, E = (4, 1024, 512, 2048, 8)
        TOP_K = 1
        CAPACITY_FACTOR = 1.25
        Bh, Lh, Dh = h.shape
        T = Bh * Lh
        capacity = max(1, math.ceil(CAPACITY_FACTOR * (T * TOP_K / E)))
        x = h.reshape(T, Dh)
        logits = x @ gate_w.T + gate_b
        probs = jax.nn.softmax(logits, axis=-1)
        idx = jnp.argmax(probs, axis=-1)
        top_prob = jnp.max(probs, axis=-1)
        one_hot = jax.nn.one_hot(idx, E, dtype=jnp.int32)
        pos = jnp.take_along_axis(jnp.cumsum(one_hot, axis=0), idx[:, None], axis=1)[:, 0] - 1
        keep = pos < capacity
        safe_pos = jnp.where(keep, pos, 0)
        buf = jnp.zeros((E, capacity, Dh), dtype=x.dtype)
        buf = buf.at[idx, safe_pos].add(x * keep[:, None].astype(x.dtype))
        hdn = jax.nn.relu(jnp.einsum('ecd,edf->ecf', buf, w1) + b1[:, None, :])
        eout = jnp.einsum('ecf,efd->ecd', hdn, w2) + b2[:, None, :]
        gathered = eout[idx, safe_pos]
        out = gathered * (top_prob * keep.astype(x.dtype))[:, None]
        return out.reshape(Bh, Lh, Dh)
    x = x + _L0_xattn_ref(_layernorm(x, axis=-1), mask_BxS_ff1, ctx_1024, mask_BxS2_ik0, L0_xattn_Ws, L0_xattn_W, L0_xattn_w, L0_xattn_b, L0_xattn_Wcw, L0_xattn_bcw, L0_xattn_Wcb, L0_xattn_bcb)
    x = x + _L0_ffn_ref(_layernorm(x, axis=-1), L0_ffn_gate_w, L0_ffn_gate_b, L0_ffn_w1, L0_ffn_b1, L0_ffn_w2, L0_ffn_b2)
    return x

_drawn_inputs = setup_inputs


def setup_inputs(seed=0):
    import zlib

    import numpy as np

    out = dict(_drawn_inputs(seed))
    spreads = {'L0_ffn_gate_b': (0.0, 0.1), 'L0_ffn_b1': (0.0, 0.726), 'L0_ffn_b2': (0.0, 0.449)}
    factors = {'L0_xattn_b': 8.0}
    for name, (base, spread) in spreads.items():
        noise = np.random.default_rng([zlib.crc32(name.encode()), seed]).standard_normal(out[name].shape)
        drawn = base * np.exp(spread * noise) if base else spread * noise
        out[name] = jnp.asarray(drawn.astype(out[name].dtype))
    for name, factor in factors.items():
        out[name] = (out[name] * factor).astype(out[name].dtype)
    return out
```

```python
import concourse.bass as bass
from concourse import mybir
from contextlib import ExitStack


def xattn_moe_kernel(nc, x, ctx, mask, Ws, W, w, b, Wcw, bcw, Wcb, bcb, gate_w, gate_b, w1, b1, w2, b2, out):
    fp32 = mybir.dt.float32
    i32 = mybir.dt.int32
    u32 = mybir.dt.uint32
    ALU = mybir.AluOpType
    ACT = mybir.ActivationFunctionType
    X = mybir.AxisListType.X
    ds = bass.ds

    P = 128
    B, S, D = x.shape
    T = ctx.shape[1]
    E, _, FF = w1.shape
    DC = D // P
    NI = S // P
    NF = FF // P
    TOK = B * S
    CAP = -(-5 * TOK // (4 * E))
    NS = CAP // P
    assert NS * P == CAP and NF % 8 == 0 and B % 2 == 0
    G = 4
    NG = -(-T // G)
    TP = NG * G
    HB_ = B // 2
    EPS = 1e-5
    NEG = 1e30
    BIG = 1.0e6
    MAGIC = 1597463007.0
    PAY = D + 4
    QF = 4
    NU = NF // QF
    CA = 3 * P
    CB = CAP - CA

    buf = nc.dram_tensor("dispatched", (E * CAP, PAY), fp32, kind="Internal").ap()
    out_rows = out.rearrange("b s d -> (b s) d")

    st = ExitStack()
    with st:
        def sb(name, shape, dt=fp32):
            return st.enter_context(nc.sbuf_tensor(name, shape, dt))

        def sem(name):
            return st.enter_context(nc.semaphore(name))

        area1 = sb("area1", [P, G * DC * S])
        area2 = sb("area2", [P, 2 * DC * S])
        area3 = sb("area3", [P, 4 * NI * D])
        Ws_sb = area1[:, 0:DC * D].rearrange("p (c e) -> p c e", c=DC)
        ctx_sb = area1[0:T, DC * D:DC * D + B * D].rearrange("p (b d) -> p b d", b=B)
        perm = area1[0:T, DC * D + B * D:DC * D + B * D + B * T].rearrange("p (b t) -> p b t", b=B)
        wc_wide = area1[:, DC * D + B * D + B * T:DC * D + B * D + B * T + 2 * DC * P].rearrange(
            "p (m c q) -> p m c q", m=2, c=DC)
        h_ring = area1[:, :].rearrange("p (t c f) -> p t c f", t=G, c=DC)
        xT = area1[:, 0:2 * DC * CAP].rearrange("p (k c n) -> p k c n", k=2, c=DC)
        y_out = area1[:, 2 * DC * CAP:2 * DC * CAP + NS * D].rearrange("p (s d) -> p s d", s=NS)
        ctxT = area2[:, 0:DC * B * T].rearrange("p (c b t) -> p c b t", c=DC, b=B)
        maskw = area2[0:T, DC * B * T:DC * B * T + B * P].rearrange("p (b q) -> p b q", b=B)
        h2 = area2[:, 0:NI * D].rearrange("p (i d) -> p i d", i=NI)
        h2T = area2[:, NI * D:2 * NI * D].rearrange("p (c f) -> p c f", c=DC)
        x_sb = [area3[:, k * NI * D:(k + 1) * NI * D].rearrange("p (i d) -> p i d", i=NI) for k in (0, 1)]
        xn = [area3[:, (2 + k) * NI * D:(3 + k) * NI * D].rearrange("p (i d) -> p i d", i=NI) for k in (0, 1)]
        xin = area3[:, 0:2 * NS * PAY].rearrange("p (k s d) -> p k s d", k=2, s=NS)
        hx = area3[:, 2 * NS * PAY:2 * NS * PAY + NS * D].rearrange("p (s d) -> p s d", s=NS)

        W_sb = sb("W_sb", [P, DC, D])
        xnT = sb("xnT", [P, DC, S])
        featT = sb("featT", [P, DC, S])
        txtT = sb("txtT", [P, DC, B, TP])
        partial = sb("partial", [P, 2, S])
        rho_rows = sb("rho_rows", [G, S])
        pay = [sb(f"pay{k}", [P, NI, PAY]) for k in (0, 1)]
        slot_idx = [sb(f"slot_idx{k}", [P, NI], u32) for k in (0, 1)]
        bias_row = sb("bias_row", [P, B, T])
        cw_row = sb("cw_row", [P, B, T])
        cb_row = sb("cb_row", [P, B, T])
        z = sb("z", [P, NI, T])
        zs = sb("zs", [P, NI, T])
        prob = sb("prob", [P, NI, T])
        pw = sb("pw", [P, 2, NI, T])
        w1q = [sb(f"w1q{k}", [P, DC, QF * P]) for k in (0, 1)]
        w2q = [sb(f"w2q{k}", [P, QF, D]) for k in (0, 1)]
        hA = [sb(f"hA{k}", [P, CA]) for k in (0, 1)]
        hB = [sb(f"hB{k}", [P, CB]) for k in (0, 1)]
        b2row = sb("b2row", [1, 2, D])
        b1rows = sb("b1rows", [E * NF, P])
        b1T = sb("b1T", [P, E * NF])
        blank = sb("blank", [P, PAY])

        ident = sb("ident", [P, P])
        triu = sb("triu", [P, P])
        ones = sb("ones", [P, P])
        onesel = sb("onesel", [P, G, G])
        wsel = sb("wsel", [P, G, G])
        w_col = sb("w_col", [P, DC])
        b_col = sb("b_col", [P, DC])
        wc_col = sb("wc_col", [P, 2, DC])
        bc_col = sb("bc_col", [P, 2])
        gwT = sb("gwT", [P, DC, E])
        gw_rows = sb("gw_rows", [E, D])
        gb_row = sb("gb_row", [P, E])
        mask_i = sb("mask_i", [T, B], i32)
        maskf = sb("maskf", [T, B])
        active = sb("active", [T, B])
        kpos = sb("kpos", [T, 4, B])
        t_index = sb("t_index", [P, 1])
        col_index = sb("col_index", [P, P])
        group_edge = sb("group_edge", [1, B, NG])
        past_edge = sb("past_edge", [1, B, NG])
        counts = sb("counts", [1, 4, B])
        ctl = sb("ctl", [1, 2, B], i32)
        erev = sb("erev", [P, E])
        ebase = sb("ebase", [P, E])
        tokid = sb("tokid", [P, NI])

        ln_st = sb("ln_st", [P, NI, 6])
        ln_mv = sb("ln_mv", [P, NI, 2])
        ln_v = sb("ln_v", [P, NI])
        ln_y = sb("ln_y", [P, NI], i32)
        ln_t = sb("ln_t", [P, 2, NI])
        mx = sb("mx", [P, NI])
        nd = sb("nd", [P, 3, NI])
        rden = sb("rden", [P, NI])
        ws_in = sb("ws_in", [P, 2, NI])
        ws = sb("ws", [P, 2, NI])
        lg = sb("lg", [P, NI, E])
        lgd = sb("lgd", [P, NI, E])
        lge = sb("lge", [P, NI, E])
        eq = sb("eq", [P, NI, E])
        onehot = sb("onehot", [P, NI, E])
        top = sb("top", [P, 2, NI])
        psum_e = sb("psum_e", [P, NI])
        run = sb("run", [P, NI + 1, E])
        cume = sb("cume", [P, 2, NI, E])
        pos = sb("pos", [P, 4, NI])
        out_idx = sb("out_idx", [P, NS], u32)

        PS = st.enter_context(nc.psum_tensor("PS", [P, 8, 512], fp32))
        bankA = [PS[:, 0, :], PS[:, 1, :]]
        bankR = PS[0:G, 2:4, :]
        bankT = PS[:, 4, :]
        bankL = PS[:, 5, :]
        bankY = PS[:, 0:NS, :]
        bankHA, bankHB, bankX = PS[:, 5, :], PS[:, 6, :], PS[:, 7, :]

        s_const = sem("const_built")
        s_ld = sem("keys_and_mask_loaded")
        s_ldw = sem("small_weights_loaded")
        s_ldW = sem("W_loaded")
        s_x = [sem(f"x_loaded_{k}") for k in (0, 1)]
        s_blank = sem("slots_blanked")
        s_pre = sem("prelude_dve_step")
        s_preA = sem("prelude_bank_filled")
        s_preF = sem("prelude_bank_read")
        s_preA2 = sem("attended_keys_counted")
        s_perm = sem("permutations_built")
        s_wide = sem("wide_columns_built")
        s_ctl = sem("group_counts_ready")
        s_ln = sem("ln_chain")
        s_xn = sem("xn_ready")
        s_afull = sem("bankA_filled")
        s_afree = sem("bankA_read")
        s_h = sem("tanh_ready")
        s_sum = sem("partial_ready")
        s_gch = sem("partial_chain")
        s_hfree = sem("rho_key_done")
        s_rfree = sem("bankR_read")
        s_row = sem("rho_group_transposed")
        s_ep = sem("epilogue_chain")
        s_zs = sem("scores_shifted")
        s_exp = sem("exp_done")
        s_wsin = sem("gates_in_ready")
        s_ws = sem("gates_ready")
        s_x2 = sem("x2_ready")
        s_h2 = sem("h2_ready")
        s_log = sem("logits_ready")
        s_lgd = sem("logits_shifted")
        s_lge = sem("logits_exp_done")
        s_oh = sem("onehot_ready")
        s_cnt = sem("expert_counts_ready")
        s_slot = sem("slots_ready")
        s_store = [sem(f"x2_stored_{k}") for k in (0, 1)]
        s_scat = sem("rows_dispatched")
        s_payfree = sem("payload_dispatched")
        s_yfree = sem("expert_buffer_written_out")
        s_w = [sem(f"weight_unit_loaded_{k}") for k in (0, 1)]
        s_b2 = sem("b2_loaded")
        s_xin = sem("expert_rows_loaded")
        s_hx = sem("expert_rows_normalised")
        s_xf = sem("bankX_filled")
        s_xe = sem("bankX_read")
        s_upA = sem("hidden_A_in_psum")
        s_upB = sem("hidden_B_in_psum")
        s_hA = sem("hidden_A_ready")
        s_hB = sem("hidden_B_ready")
        s_dnA = sem("hidden_A_used")
        s_dnB = sem("hidden_B_used")
        s_yr = sem("expert_output_read")
        s_oidx = sem("token_numbers_ready")
        s_yo = sem("expert_rows_written")

        def z_half(rows, hf):
            return rows[:, hf * HB_:(hf + 1) * HB_, :].rearrange("p b t -> p (b t)")

        PRE_FILLS = B + 2 + 4 + 2 * DC + 2
        EPI_STEPS = 39

        LN_STEPS = 13

        def wait_apart(engine, semaphore, value):
            value = value if isinstance(value, int) else engine.to_reg(value)
            engine.wait_ge(s_const, 1)
            engine.wait_ge(semaphore, value)

        block = st.enter_context(nc.Block())

        @block.sync
        def _(sp):
            sp.dma_start(mask_i[:, :], mask.rearrange("b t -> t b"), allow_slow_non_contiguous=True).then_inc(s_ld, 16)
            sp.dma_start(ctx_sb, ctx.rearrange("b t d -> t b d")).then_inc(s_ld, 16)
            for k in (0, 1):
                sp.dma_start(x_sb[k], x[k].rearrange("(i p) d -> p i d", p=P)).then_inc(s_x[k], 16)
            sp.dma_start(Ws_sb, Ws.rearrange("(c p) e -> p c e", p=P)).then_inc(s_ld, 16)
            sp.dma_start(W_sb[:, :, :], W.rearrange("(c p) e -> p c e", p=P)).then_inc(s_ldW, 16)

            def load_unit(j, k, e, q):
                sp.dma_start(w1q[k][:, :, :], w1[e, :, :].rearrange("(c p) f -> p c f", p=P)
                             [:, :, q * QF * P:(q + 1) * QF * P]).then_inc(s_w[k], 16)
                sp.dma_start(w2q[k][:, :, :], w2[e, :, :].rearrange("(g p) d -> p g d", p=P)
                             [:, q * QF:(q + 1) * QF, :]).then_inc(s_w[k], 16)

            def batch(bb, k, last):
                sp.wait_ge(s_x2, bb + 1)
                if not last:
                    sp.dma_start(x_sb[k], x[bb + 2].rearrange("(i p) d -> p i d", p=P)).then_inc(s_x[k], 16)
                sp.dma_start(out[bb].rearrange("(i p) d -> p i d", p=P), pay[k][:, :, 0:D]).then_inc(s_store[k], 16)

            load_unit(0, 0, 0, 0)
            load_unit(1, 1, 0, 1)
            with sp.Fori(0, HB_ - 1) as i:
                for k in (0, 1):
                    batch(2 * i + k, k, False)
            for k in (0, 1):
                batch(B - 2 + k, k, True)

            def load_rows(e, kk):
                sp.dma_start(xin[:, kk, :, :] if isinstance(kk, int) else xin[:, ds(kk, 1), :, :].rearrange("p k s d -> p (k s) d"),
                             buf[ds(e * CAP, CAP), :].rearrange("(s p) d -> p s d", p=P)).then_inc(s_xin, 16)

            def load_b2(e, kk):
                sp.dma_start(b2row[0:1, ds(kk, 1), :].rearrange("p k d -> p (k d)"), b2[ds(e, 1), :]).then_inc(s_b2, 16)

            sp.wait_ge(s_slot, B)
            sp.wait_ge(s_scat, B * NI * 16)
            load_rows(0, 0)
            load_b2(0, 0)

            def expert(e, last):
                for q in range(NU):
                    j = e * NU + q + 2
                    if last and q >= NU - 2:
                        break
                    sp.wait_ge(s_dnB, (e * NU + q + 1) * QF + 2)
                    if q < NU - 2:
                        load_unit_dyn(e, q + 2, q % 2)
                    else:
                        load_unit_dyn(e + 1, q + 2 - NU, q % 2)
                    if q == 0 and not last:
                        sp.wait_ge(s_yr, e * NS + 1)
                        load_rows(e + 1, (e + 1) % 2)
                        load_b2(e + 1, (e + 1) % 2)

            def load_unit_dyn(e, q, k):
                sp.dma_start(w1q[k][:, :, :], w1[ds(e, 1), :, q * QF * P:(q + 1) * QF * P]
                             .rearrange("e (c p) f -> p (e c) f", p=P)).then_inc(s_w[k], 16)
                sp.dma_start(w2q[k][:, :, :], w2[ds(e, 1), q * QF * P:(q + 1) * QF * P, :]
                             .rearrange("e (g p) d -> p (e g) d", p=P)).then_inc(s_w[k], 16)

            with sp.Fori(0, E - 1) as e:
                expert(e, False)
            expert(E - 1, True)
            for k in (0, 1):
                sp.wait_ge(s_store[k], HB_ * 16 + 16)
            sp.wait_ge(s_yo, E * NS * 16)
            sp.wait_ge(s_blank, 16)

        @block.gpsimd
        def _(pool):
            pool.memset(ones[:, :], 1.0).then_inc(s_const, 1)
            pool.memset(ident[:, :], 0.0).then_inc(s_const, 1)
            pool.memset(blank[:, :], 0.0).then_inc(s_const, 1)
            pool.memset(onesel[:, :, :], 0.0).then_inc(s_const, 1)
            pool.memset(txtT[:, :, :, T:TP], 0.0).then_inc(s_const, 1)
            pool.memset(run[:, :, :], 0.0).then_inc(s_const, 1)
            pool.iota(col_index[:, :], pattern=[[1, P]], base=0, channel_multiplier=0,
                      allow_small_or_imprecise_dtypes=True).then_inc(s_const, 1)
            pool.iota(t_index[:, :], pattern=[[0, 1]], base=0, channel_multiplier=1,
                      allow_small_or_imprecise_dtypes=True).then_inc(s_const, 1)
            pool.iota(group_edge[:, :, :], pattern=[[0, B], [G, NG]], base=0, channel_multiplier=0,
                      allow_small_or_imprecise_dtypes=True).then_inc(s_const, 1)
            pool.iota(erev[:, :], pattern=[[-1, E]], base=E, channel_multiplier=0,
                      allow_small_or_imprecise_dtypes=True).then_inc(s_const, 1)
            pool.iota(ebase[:, :], pattern=[[CAP, E]], base=0, channel_multiplier=0,
                      allow_small_or_imprecise_dtypes=True).then_inc(s_const, 1)
            pool.iota(tokid[:, :], pattern=[[P, NI]], base=0, channel_multiplier=1,
                      allow_small_or_imprecise_dtypes=True).then_inc(s_const, 1)
            pool.wait_ge(s_const, 12)
            pool.affine_select(out=ident[:, :], in_=ident[:, :], compare_op=ALU.not_equal, fill=1.0,
                               base=0, pattern=[[-1, P]], channel_multiplier=1).then_inc(s_const, 1)
            pool.affine_select(out=triu[:, :], in_=ones[:, :], compare_op=ALU.is_ge, fill=0.0,
                               base=0, pattern=[[1, P]], channel_multiplier=-1).then_inc(s_const, 1)
            pool.affine_select(out=onesel[:, :, :], in_=onesel[:, :, :], compare_op=ALU.not_equal, fill=1.0,
                               base=0, pattern=[[1, G], [-1, G]], channel_multiplier=0).then_inc(s_const, 1)
            pool.memset(blank[:, PAY - 1:PAY], BIG).then_inc(s_const, 1)
            pool.wait_ge(s_const, 16)
            pool.dma_start(buf.rearrange("(s p) d -> p s d", p=P),
                           blank[:, None, :].broadcast_to([P, E * NS, PAY])).then_inc(s_blank, 16)
            pool.sem_inc(s_payfree, 2)
            for k in (0, 1):
                pool.sem_inc(s_store[k], 16)
            pool.sem_inc(s_yfree, 1)
            pool.wait_ge(s_blank, 16)

            def batch(bb, k):
                wait_apart(pool, s_slot, bb + 1)
                for i in range(NI):
                    pool.indirect_dma_start(buf, bass.IndirectOffsetOnAxis(ap=slot_idx[k][:, i:i + 1], axis=0),
                                            pay[k][:, i, :], None, bounds_check=E * CAP - 1,
                                            oob_is_err=False).then_inc(s_scat, 16)
                pool.wait_ge(s_scat, (bb + 1) * NI * 16)
                pool.sem_inc(s_payfree, 1)

            with pool.Fori(0, HB_) as i:
                for k in (0, 1):
                    batch(2 * i + k, k)

            for k in (0, 1):
                pool.wait_ge(s_store[k], HB_ * 16 + 16)
            with pool.Fori(0, E) as e:
                for s in range(NS):
                    wait_apart(pool, s_yr, e * NS + s + 2)
                    pool.indirect_dma_start(out_rows, bass.IndirectOffsetOnAxis(ap=out_idx[:, s:s + 1], axis=0),
                                            y_out[:, s, :], None, bounds_check=TOK - 1,
                                            oob_is_err=False).then_inc(s_yo, 16)
                pool.wait_ge(s_yo, (e + 1) * NS * 16)
                pool.sem_inc(s_yfree, 1)

        @block.scalar
        def _(act):
            act.dma_start(gw_rows[:, :], gate_w).then_inc(s_ldw, 16)
            act.dma_start(b1rows[:, :], b1.rearrange("e (f p) -> (e f) p", p=P)).then_inc(s_ldw, 16)
            act.dma_start(w_col[:, :], w.rearrange("(c p) o -> p (c o)", p=P),
                          allow_slow_non_contiguous=True).then_inc(s_ldw, 16)
            act.dma_start(b_col[:, :], b.rearrange("o (c p) -> p (o c)", p=P),
                          allow_slow_non_contiguous=True).then_inc(s_ldw, 16)
            act.dma_start(wc_col[:, 0, :], Wcw.rearrange("o (c p) -> p (o c)", p=P),
                          allow_slow_non_contiguous=True).then_inc(s_ldw, 16)
            act.dma_start(wc_col[:, 1, :], Wcb.rearrange("o (c p) -> p (o c)", p=P),
                          allow_slow_non_contiguous=True).then_inc(s_ldw, 16)
            act.dma_start(bc_col[:, 0:1], bcw.rearrange("(a o) -> a o", a=1).broadcast_to([P, 1])).then_inc(s_ldw, 16)
            act.dma_start(bc_col[:, 1:2], bcb.rearrange("(a o) -> a o", a=1).broadcast_to([P, 1])).then_inc(s_ldw, 16)
            act.dma_start(gb_row[:, :], gate_b.rearrange("(a o) -> a o", a=1).broadcast_to([P, E])).then_inc(s_ldw, 16)

            f = 0

            def filled():
                nonlocal f
                f += 1
                act.wait_ge(s_preA, f)

            for n in range(B):
                filled()
                act.activation(ctxT[:, :, n, :], bankA[(f - 1) % 2][:, 0:DC * T].rearrange("p (c t) -> p c t", c=DC),
                               ACT.Copy).then_inc(s_preF, 1)
            for hf in (0, 1):
                filled()
                act.activation(z_half(bias_row, hf), bankA[(f - 1) % 2][:, 0:HB_ * T], ACT.Copy).then_inc(s_preF, 1)
            for which in (cw_row, cb_row):
                for hf in (0, 1):
                    filled()
                    act.activation(z_half(which, hf), bankA[(f - 1) % 2][:, 0:HB_ * T], ACT.Copy).then_inc(s_preF, 1)
            act.wait_ge(s_ldw, 9 * 16)
            for c in range(DC):
                for hf in (0, 1):
                    filled()
                    act.activation(txtT[:, c, hf * HB_:(hf + 1) * HB_, 0:T],
                                   bankA[(f - 1) % 2][:, 0:HB_ * T].rearrange("p (b t) -> p b t", b=HB_),
                                   ACT.Identity, bias=b_col[:, c:c + 1]).then_inc(s_preF, 1)
            filled()
            act.activation(gwT[:, :, :], bankA[(f - 1) % 2][:, 0:DC * E].rearrange("p (c e) -> p c e", c=DC),
                           ACT.Copy).then_inc(s_preF, 1)
            filled()
            act.activation(b1T[:, :], bankA[(f - 1) % 2][:, 0:E * NF], ACT.Copy).then_inc(s_preF, 1)
            assert f == PRE_FILLS

            def feat_evacs(base):
                for c in range(DC):
                    act.wait_ge(s_afull, base + c + 1)
                    act.activation(xnT[:, c, :], bankA[c % 2], ACT.Copy).then_inc(s_afree, 1)

            def proj_evacs(base):
                for c in range(DC):
                    act.wait_ge(s_afull, base + DC + c + 1)
                    act.activation(featT[:, c, :], bankA[c % 2], ACT.Copy).then_inc(s_afree, 1)

            feat_evacs(0)
            proj_evacs(0)
            act.wait_ge(s_afree, 2 * DC)
            act.wait_ge(s_preF, PRE_FILLS)
            act.wait_ge(s_ctl, 1)

            def batch(bb, last):
                n = act.value_load(ctl[0:1, 0, ds(bb, 1)], min_val=1, max_val=NG)
                k0 = act.value_load(ctl[0:1, 1, ds(bb, 1)], min_val=0, max_val=B * NG)
                with act.Fori(0, n) as g:
                    for t in range(G):
                        wait_apart(act, s_hfree, (k0 + g) * G + t + 1)
                        for c in range(DC):
                            ins = act.activation(h_ring[:, t, c, :], featT[:, c, :], ACT.Tanh,
                                                 bias=txtT[:, c, ds(bb, 1), ds(g * G + t, 1)].rearrange("p b t -> p (b t)"))
                        ins.then_inc(s_h, 1)
                base = 2 * DC + bb * 3 * DC
                if not last:
                    feat_evacs(base)
                act.wait_ge(s_zs, bb + 1)
                act.activation(prob[:, :, :], zs[:, :, :], ACT.Exp).then_inc(s_exp, 1)
                act.wait_ge(s_wsin, bb + 1)
                for m in (0, 1):
                    act.activation(ws[:, m, :], ws_in[:, m, :], ACT.Tanh, bias=bc_col[:, m:m + 1]).then_inc(s_ws, 1)
                if not last:
                    proj_evacs(base)
                    base = base + 2 * DC
                for c in range(DC):
                    act.wait_ge(s_afull, base + c + 1)
                    act.activation(h2T[:, c, :], bankA[c % 2], ACT.Copy).then_inc(s_afree, 1)
                act.wait_ge(s_lgd, bb + 1)
                act.activation(lge[:, :, :], lgd[:, :, :], ACT.Exp).then_inc(s_lge, 1)
                if not last:
                    act.wait_ge(s_afree, base + DC)

            with act.Fori(0, B - 1) as bb:
                batch(bb, False)
            batch(B - 1, True)

            def step(j, s):
                wait_apart(act, s_upA, j + 1)
                act.wait_ge(s_dnA, j + 1)
                act.activation(hA[s % 2][:, :], bankHA[:, 0:CA], ACT.Relu,
                               bias=b1T[:, ds(j, 1)]).then_inc(s_hA, 1)
                wait_apart(act, s_upB, j + 1)
                act.wait_ge(s_dnB, j + 1)
                act.activation(hB[s % 2][:, :], bankHB[:, 0:CB], ACT.Relu,
                               bias=b1T[:, ds(j, 1)]).then_inc(s_hB, 1)

            with act.Fori(0, E * NF // 2) as j2:
                for s in (0, 1):
                    step(2 * j2 + s, s)

        @block.vector
        def _(dve):
            def wait(engine, semaphore, value):
                engine.wait_ge(semaphore, value)

            class Chain:

                def __init__(self, semaphore, base):
                    self.semaphore, self.base, self.n = semaphore, base, 0

                def link(self, ins, apart=False):
                    self.n += 1
                    ins.then_inc(self.semaphore, 1)
                    (wait_apart if apart else wait)(dve, self.semaphore, self.base + self.n)

            dve.sem_inc(s_rfree, 2)
            dve.sem_inc(s_hfree, G)
            dve.sem_inc(s_yr, 1)
            dve.sem_inc(s_dnA, 2)
            dve.sem_inc(s_dnB, 2)

            pre = Chain(s_pre, 0)
            dve.wait_ge(s_ld, 3 * 16)
            dve.wait_ge(s_const, 16)
            pre.link(dve.tensor_copy(maskf[:, :], mask_i[:, :]))
            pre.link(dve.tensor_scalar(active[:, :], maskf[:, :], 0.0, None, ALU.is_gt))
            dve.wait_ge(s_preA2, 1)
            cnt_cum, cnt_all = bankT[0:T, 0:B], bankT[:, B:2 * B]
            pre.link(dve.tensor_copy(kpos[:, 3, :], cnt_cum))
            pre.link(dve.scalar_tensor_tensor(kpos[:, 0, :], bankT[0:T, B:2 * B], t_index[0:T, 0:1], kpos[:, 3, :],
                                              ALU.add, ALU.subtract))
            pre.link(dve.scalar_tensor_tensor(kpos[:, 1, :], kpos[:, 3, :], -1.0, kpos[:, 0, :],
                                              ALU.add, ALU.subtract))
            pre.link(dve.tensor_tensor(kpos[:, 2, :], kpos[:, 1, :], active[:, :], ALU.mult))
            pre.link(dve.tensor_tensor(kpos[:, 3, :], kpos[:, 2, :], kpos[:, 0, :], ALU.add))
            for n in range(B):
                dve.tensor_scalar(maskw[:, n, :], ones[0:T, :], maskf[:, n:n + 1], None, ALU.mult)
                ins = dve.tensor_scalar(perm[:, n, :], col_index[0:T, 0:T], kpos[:, 3, n:n + 1], None, ALU.is_equal)
            ins.then_inc(s_perm, 1)
            pre.link(dve.tensor_copy(counts[:, 0, :], bankT[0:1, B:2 * B]))
            pre.link(dve.tensor_tensor(past_edge[:, :, :], counts[:, 0, :][:, :, None].broadcast_to([1, B, NG]),
                                       group_edge[:, :, :], ALU.is_gt))
            pre.link(dve.tensor_reduce(counts[:, 1, :], past_edge[:, :, :], X, ALU.add))
            pre.link(dve.tensor_scalar(counts[:, 1, :], counts[:, 1, :], 1.0, None, ALU.max))
            pre.link(dve.tensor_tensor_scan(counts[:, 2, :], ones[0:1, 0:B], counts[:, 1, :], 0.0,
                                            ALU.mult, ALU.add))
            pre.link(dve.tensor_tensor(counts[:, 3, :], counts[:, 2, :], counts[:, 1, :], ALU.subtract))
            pre.link(dve.tensor_copy(ctl[:, 0, :], counts[:, 1, :]))
            pre.link(dve.tensor_copy(ctl[:, 1, :], counts[:, 3, :]))
            dve.nop().then_inc(s_ctl, 1)
            pre.link(dve.memset(bankT, 0.0))
            dve.wait_ge(s_ldw, 9 * 16)
            for m in (0, 1):
                for c in range(DC):
                    dve.tensor_scalar(wc_wide[:, m, c, :], ones[:, :], wc_col[:, m, c:c + 1], None, ALU.mult)
            dve.tensor_scalar(wsel[:, :, :], onesel[:, :, :], w_col[:, 0:1], None, ALU.mult).then_inc(s_wide, 1)

            def rsqrt(chain, var):
                y = ln_y[:, :].bitcast(fp32)
                chain.link(dve.tensor_scalar(ln_v[:, :], var, EPS, None, ALU.add))
                chain.link(dve.tensor_scalar(ln_y[:, :], ln_v[:, :].bitcast(i32), -0.5, MAGIC, ALU.mult, ALU.add))
                for _ in range(3):
                    chain.link(dve.tensor_tensor(ln_t[:, 0, :], y, y, ALU.mult))
                    chain.link(dve.scalar_tensor_tensor(ln_t[:, 1, :], ln_t[:, 0, :], -0.5, ln_v[:, :],
                                                        ALU.mult, ALU.mult))
                    chain.link(dve.scalar_tensor_tensor(y, ln_t[:, 1, :], 1.5, y, ALU.add, ALU.mult))
                return y

            def moments(chain, src):
                for i in range(NI - 1):
                    dve.bn_stats(ln_st[:, i, :], src(i))
                chain.link(dve.bn_stats(ln_st[:, NI - 1, :], src(NI - 1)), True)
                for i in range(NI - 1):
                    dve.bn_aggr(ln_mv[:, i, :], ln_st[:, i, :])
                chain.link(dve.bn_aggr(ln_mv[:, NI - 1, :], ln_st[:, NI - 1, :]))

            def ln1(ib, k):
                chain = Chain(s_ln, (2 * ib + k) * LN_STEPS)
                dve.wait_ge(s_x[k], (ib + 1) * 16)
                moments(chain, lambda i: x_sb[k][:, i, :])
                y = rsqrt(chain, ln_mv[:, :, 1])
                for i in range(NI):
                    ins = dve.tensor_scalar(xn[k][:, i, :], x_sb[k][:, i, :], ln_mv[:, i, 0:1], y[:, i:i + 1],
                                            ALU.subtract, ALU.mult)
                ins.then_inc(s_xn, 1)
                assert chain.n == LN_STEPS

            ln1(0, 0)
            ln1(0, 1)
            dve.wait_ge(s_preF, B + 2)
            pre.link(dve.tensor_scalar(bias_row[:, :, :], bias_row[:, :, :], -1.0, NEG, ALU.add, ALU.mult))
            dve.wait_ge(s_preF, B + 6)

            def groups(bb):
                n = dve.value_load(ctl[0:1, 0, ds(bb, 1)], min_val=1, max_val=NG)
                k0 = dve.value_load(ctl[0:1, 1, ds(bb, 1)], min_val=0, max_val=B * NG)
                with dve.Fori(0, n) as g:
                    kk = k0 + g
                    for t in range(G):
                        dve.wait_ge(s_h, kk * G + t + 1)
                        dve.wait_ge(s_hfree, kk * G + t + 3)
                        chain = Chain(s_gch, kk * 2 * G + 2 * t)
                        part = partial[:, t % 2, :]
                        chain.link(dve.tensor_scalar(part, h_ring[:, t, 1, :], w_col[:, 1:2], None, ALU.mult))
                        chain.link(dve.scalar_tensor_tensor(part, h_ring[:, t, 2, :], w_col[:, 2:3], part,
                                                            ALU.mult, ALU.add))
                        dve.scalar_tensor_tensor(part, h_ring[:, t, 3, :], w_col[:, 3:4], part,
                                                 ALU.mult, ALU.add).then_inc(s_sum, 1)
                    dve.wait_ge(s_hfree, kk * G + G + G)
                    dve.wait_ge(s_row, kk + 1)
                    dve.tensor_copy(rho_rows[:, :], bankR[:, ds(kk % 2, 1), :].rearrange("p a f -> p (a f)"))\
                       .then_inc(s_rfree, 1)
                dve.wait_ge(s_row, k0 + n + 1)

            def epilogue(ib, k, last):
                bb = 2 * ib + k
                ep = Chain(s_ep, bb * EPI_STEPS)
                rT = bankT.rearrange("p (i t) -> p i t", i=NI)[:, :, 0:T]

                def key_row(r):
                    return r[:, ds(bb, 1), :].broadcast_to([P, NI, T])

                ep.link(dve.tensor_tensor(z[:, :, :], rT, key_row(bias_row), ALU.add))
                ep.link(dve.tensor_reduce(mx[:, :], z[:, :, :], X, ALU.max))
                dve.tensor_tensor(zs[:, :, :], z[:, :, :], mx[:, :][:, :, None].broadcast_to([P, NI, T]),
                                  ALU.subtract).then_inc(s_zs, 1)
                dve.wait_ge(s_exp, bb + 1)
                dve.tensor_reduce(nd[:, 0, :], prob[:, :, :], X, ALU.add)
                ep.link(dve.tensor_tensor(pw[:, 0, :, :], prob[:, :, :], key_row(cw_row), ALU.mult))
                ep.link(dve.tensor_tensor(pw[:, 1, :, :], prob[:, :, :], key_row(cb_row), ALU.mult))
                dve.reciprocal(rden[:, :], nd[:, 0, :])
                ep.link(dve.tensor_reduce(nd[:, 1:3, :], pw[:, :, :, :], X, ALU.add))
                dve.tensor_tensor(ws_in[:, :, :], nd[:, 1:3, :], rden[:, None, :].broadcast_to([P, 2, NI]),
                                  ALU.mult).then_inc(s_wsin, 1)
                dve.wait_ge(s_payfree, bb + 1)
                dve.wait_ge(s_store[k], ib * 16 + 16)
                dve.wait_ge(s_ws, 2 * bb + 2)
                for i in range(NI):
                    ins = dve.tensor_scalar(pay[k][:, i, 0:D], xn[k][:, i, :], ws[:, 0, i:i + 1], ws[:, 1, i:i + 1],
                                            ALU.mult, ALU.add)
                ep.link(ins)
                for i in range(NI):
                    ins = dve.tensor_tensor(pay[k][:, i, 0:D], pay[k][:, i, 0:D], x_sb[k][:, i, :], ALU.add)
                ep.link(ins)
                dve.nop().then_inc(s_x2, 1)
                moments(ep, lambda i: pay[k][:, i, 0:D])
                y = rsqrt(ep, ln_mv[:, :, 1])
                for i in range(NI):
                    ins = dve.tensor_scalar(h2[:, i, :], pay[k][:, i, 0:D], ln_mv[:, i, 0:1], y[:, i:i + 1],
                                            ALU.subtract, ALU.mult)
                ins.then_inc(s_h2, 1)
                dve.tensor_copy(pay[k][:, :, D], ln_mv[:, :, 0])
                dve.tensor_copy(pay[k][:, :, D + 1], y)
                dve.tensor_copy(pay[k][:, :, D + 3], tokid[:, :])
                ep.link(dve.tensor_scalar(pos[:, 3, :], tokid[:, :], float(S), None, ALU.add))
                ep.link(dve.tensor_copy(tokid[:, :], pos[:, 3, :]))
                if not last:
                    ln1(ib + 1, k)
                dve.wait_ge(s_log, bb + 1)
                ep.link(dve.tensor_tensor(lg[:, :, :], bankL[:, 0:NI * E].rearrange("p (i e) -> p i e", i=NI),
                                          gb_row[:, None, :].broadcast_to([P, NI, E]), ALU.add))
                ep.link(dve.tensor_reduce(top[:, 0, :], lg[:, :, :], X, ALU.max))
                top_wide = top[:, 0, :][:, :, None].broadcast_to([P, NI, E])
                dve.tensor_tensor(lgd[:, :, :], lg[:, :, :], top_wide, ALU.subtract).then_inc(s_lgd, 1)
                ep.link(dve.tensor_tensor(eq[:, :, :], lg[:, :, :], top_wide, ALU.is_equal))
                ep.link(dve.tensor_tensor(eq[:, :, :], eq[:, :, :], erev[:, None, :].broadcast_to([P, NI, E]), ALU.mult))
                ep.link(dve.tensor_reduce(top[:, 1, :], eq[:, :, :], X, ALU.max))
                dve.tensor_tensor(onehot[:, :, :], eq[:, :, :], top[:, 1, :][:, :, None].broadcast_to([P, NI, E]),
                                  ALU.is_equal).then_inc(s_oh, 1)
                dve.wait_ge(s_lge, bb + 1)
                ep.link(dve.tensor_reduce(psum_e[:, :], lge[:, :, :], X, ALU.add))
                dve.reciprocal(pay[k][:, :, D + 2], psum_e[:, :])
                dve.wait_ge(s_cnt, bb + 1)
                cnt = bankL[:, 64:64 + NI * E].rearrange("p (i e) -> p i e", i=NI)
                tot = bankL[:, 128:128 + NI * E].rearrange("p (i e) -> p i e", i=NI)
                ep.link(dve.tensor_copy(run[:, 0, :], run[:, NI, :]))
                for i in range(NI):
                    ep.link(dve.tensor_tensor(run[:, i + 1, :], run[:, i, :], tot[:, i, :], ALU.add))
                ep.link(dve.tensor_tensor(cume[:, 0, :, :], cnt, run[:, 0:NI, :], ALU.add))
                ep.link(dve.tensor_tensor(cume[:, 0, :, :], cume[:, 0, :, :], onehot[:, :, :], ALU.mult))
                ep.link(dve.tensor_tensor(cume[:, 1, :, :], onehot[:, :, :],
                                          ebase[:, None, :].broadcast_to([P, NI, E]), ALU.mult))
                ep.link(dve.tensor_reduce(pos[:, 0:2, :], cume[:, :, :, :], X, ALU.add))
                ep.link(dve.tensor_scalar(pos[:, 2, :], pos[:, 0, :], float(CAP), BIG, ALU.is_gt, ALU.mult))
                ep.link(dve.scalar_tensor_tensor(pos[:, 3, :], pos[:, 0, :], -1.0, pos[:, 1, :], ALU.add, ALU.add))
                dve.tensor_tensor(slot_idx[k][:, :], pos[:, 3, :], pos[:, 2, :], ALU.add).then_inc(s_slot, 1)
                assert ep.n == EPI_STEPS, ep.n

            dve.sem_inc(s_row, 1)
            with dve.Fori(0, HB_ - 1) as i:
                for k in (0, 1):
                    groups(2 * i + k)
                    epilogue(i, k, False)
            for k in (0, 1):
                groups(B - 2 + k)
                epilogue(HB_ - 1, k, True)

            def rows_of(e, kk):
                return xin[:, ds(kk, 1), :, :].rearrange("p k s d -> p (k s) d")

            def prepare(e, kk):
                dve.wait_ge(s_xin, (e + 1) * 16)
                rows = rows_of(e, kk)
                for s in range(NS):
                    dve.tensor_scalar(hx[:, s, :], rows[:, s, 0:D], rows[:, s, D:D + 1], rows[:, s, D + 1:D + 2],
                                      ALU.subtract, ALU.mult).then_inc(s_hx, 1)
                for s in range(NS):
                    dve.wait_ge(s_xf, e * NS + s + 1)
                    dve.tensor_copy(xT[:, ds(kk, 1), :, s * P:(s + 1) * P].rearrange("p k c n -> p (k c) n"),
                                    bankX.rearrange("p (c n) -> p c n", c=DC)).then_inc(s_xe, 1)

            def finish(e, kk):
                dve.wait_ge(s_yfree, e + 1)
                rows = rows_of(e, kk)
                dve.tensor_copy(out_idx[:, :], rows[:, :, D + 3]).then_inc(s_oidx, 1)
                dve.wait_ge(s_oidx, e + 1)
                for s in range(NS):
                    if s in (0, 3):
                        dve.wait_ge((s_dnA, s_dnB)[s // 3], (e + 1) * NF + 2)
                    dve.scalar_tensor_tensor(y_out[:, s, :], bankY[:, s, :], rows[:, s, D + 2:D + 3], rows[:, s, 0:D],
                                             ALU.mult, ALU.add).then_inc(s_yr, 1)

            prepare(0, 0)
            with dve.Fori(0, E - 1) as e:
                prepare(e + 1, (e + 1) % 2)
                finish(e, e % 2)
            finish(E - 1, (E - 1) % 2)

        @block.tensor
        def _(pe):
            pe.wait_ge(s_const, 16)
            pe.wait_ge(s_pre, 2)
            pe.matmul(bankT[0:T, 0:B], triu[0:T, 0:T], active[:, :], start=True, stop=True)
            pe.matmul(bankT[:, B:2 * B], ones[0:T, :], active[:, :], start=True, stop=True).then_inc(s_preA2, 1)
            pe.wait_ge(s_ld, 3 * 16)
            pe.wait_ge(s_perm, 1)
            f = 0

            def bank():
                nonlocal f
                f += 1
                if f > 2:
                    pe.wait_ge(s_preF, f - 2)
                return bankA[(f - 1) % 2]

            for n in range(B):
                bk = bank()
                for c in range(DC):
                    ins = pe.matmul(bk[:, c * T:(c + 1) * T], ctx_sb[:, n, c * P:(c + 1) * P], perm[:, n, :],
                                    start=True, stop=True)
                ins.then_inc(s_preA, 1)
            for hf in (0, 1):
                bk = bank()
                for n in range(HB_):
                    ins = pe.matmul(bk[:, n * T:(n + 1) * T], maskw[:, hf * HB_ + n, :], perm[:, hf * HB_ + n, :],
                                    start=True, stop=True)
                ins.then_inc(s_preA, 1)

            def keys(c, hf):
                return ctxT[:, c, hf * HB_:(hf + 1) * HB_, :].rearrange("p b t -> p (b t)")

            pe.wait_ge(s_wide, 1)
            pe.wait_ge(s_preF, B)
            for m in (0, 1):
                for hf in (0, 1):
                    bk = bank()
                    for c in range(DC):
                        ins = pe.matmul(bk[:, 0:HB_ * T], wc_wide[:, m, c, :], keys(c, hf),
                                        start=(c == 0), stop=(c == DC - 1))
                    ins.then_inc(s_preA, 1)
            for c2 in range(DC):
                for hf in (0, 1):
                    bk = bank()
                    for c in range(DC):
                        ins = pe.matmul(bk[:, 0:HB_ * T], Ws_sb[:, c, c2 * P:(c2 + 1) * P], keys(c, hf),
                                        start=(c == 0), stop=(c == DC - 1))
                    ins.then_inc(s_preA, 1)
            bk = bank()
            pe.wait_ge(s_ldw, 9 * 16)
            for c in range(DC):
                ins = pe.transpose(bk[:, c * E:(c + 1) * E], gw_rows[:, c * P:(c + 1) * P], ident[0:E, 0:E])
            ins.then_inc(s_preA, 1)
            bk = bank()
            pe.transpose(bk[:, 0:E * NF], b1rows[:, :], ident[:, :]).then_inc(s_preA, 1)
            assert f == PRE_FILLS
            pe.wait_ge(s_preF, PRE_FILLS)

            def take(u, first=False):
                if not first:
                    pe.wait_ge(s_afree, u - 1)

            def features(base, k, bb, first):
                pe.wait_ge(s_xn, bb + 1)
                for c in range(DC):
                    take(base + c, first and c < 2)
                    for i in range(NI):
                        ins = pe.transpose(bankA[c % 2][:, i * P:(i + 1) * P], xn[k][:, i, c * P:(c + 1) * P], ident[:, :])
                    ins.then_inc(s_afull, 1)
                for c2 in range(DC):
                    take(base + DC + c2)
                    for c in range(DC):
                        if c2 == 0:
                            pe.wait_ge(s_afree, base + c + 1)
                        ins = pe.matmul(bankA[c2 % 2], W_sb[:, c, c2 * P:(c2 + 1) * P], xnT[:, c, :],
                                        start=(c == 0), stop=(c == DC - 1))
                    ins.then_inc(s_afull, 1)

            pe.wait_ge(s_ldW, 16)
            features(0, 0, 0, True)
            pe.wait_ge(s_ctl, 1)

            def batch(bb, k, last):
                n = pe.value_load(ctl[0:1, 0, ds(bb, 1)], min_val=1, max_val=NG)
                k0 = pe.value_load(ctl[0:1, 1, ds(bb, 1)], min_val=0, max_val=B * NG)
                with pe.Fori(0, n) as g:
                    kk = k0 + g
                    pe.wait_ge(s_rfree, kk + 1)
                    bk = bankR[:, ds(kk % 2, 1), :].rearrange("p a f -> p (a f)")
                    for t in range(G):
                        wait_apart(pe, s_h, kk * G + t + 1)
                        pe.matmul(bk, wsel[:, t, :], h_ring[:, t, 0, :], start=(t == 0), stop=False)
                        wait_apart(pe, s_sum, kk * G + t + 1)
                        pe.matmul(bk, onesel[:, t, :], partial[:, t % 2, :], start=False,
                                  stop=(t == G - 1)).then_inc(s_hfree, 1)
                    wait_apart(pe, s_rfree, kk + 3)
                    for i in range(NI):
                        ins = pe.matmul(bankT[:, ds(g * G + i * P, G)], rho_rows[:, i * P:(i + 1) * P],
                                        ident[0:G, 0:G], start=True, stop=True)
                    ins.then_inc(s_row, 1)
                base = 2 * DC + bb * 3 * DC
                if not last:
                    features(base, 1 - k, bb + 1, False)
                    base = base + 2 * DC
                pe.wait_ge(s_h2, bb + 1)
                for c in range(DC):
                    take(base + c)
                    for i in range(NI):
                        ins = pe.transpose(bankA[c % 2][:, i * P:(i + 1) * P], h2[:, i, c * P:(c + 1) * P], ident[:, :])
                    ins.then_inc(s_afull, 1)
                pe.wait_ge(s_afree, base + DC)
                for i in range(NI):
                    for c in range(DC):
                        ins = pe.matmul(bankL[:, i * E:(i + 1) * E], h2T[:, c, i * P:(i + 1) * P], gwT[:, c, :],
                                        start=(c == 0), stop=(c == DC - 1))
                ins.then_inc(s_log, 1)
                pe.wait_ge(s_oh, bb + 1)
                oh = onehot[:, :, :].rearrange("p i e -> p (i e)")
                pe.matmul(bankL[:, 64:64 + NI * E], triu[:, :], oh, start=True, stop=True)
                pe.matmul(bankL[:, 128:128 + NI * E], ones[:, :], oh, start=True, stop=True).then_inc(s_cnt, 1)

            with pe.Fori(0, HB_ - 1) as i:
                for k in (0, 1):
                    batch(2 * i + k, k, False)
            batch(B - 2, 0, False)
            batch(B - 1, 1, True)
            pe.wait_ge(s_slot, B)

            def transposes(e):
                for s in range(NS):
                    pe.wait_ge(s_hx, e * NS + s + 1)
                    if not (isinstance(e, int) and e == 0 and s == 0):
                        pe.wait_ge(s_xe, e * NS + s)
                    for c in range(DC):
                        ins = pe.transpose(bankX[:, c * P:(c + 1) * P], hx[:, s, c * P:(c + 1) * P], ident[:, :])
                    ins.then_inc(s_xf, 1)

            def up(e, s, half, first=False):
                k = (s // QF) % 2
                j = e * NF + s
                if s == 0 and half == 0:
                    pe.wait_ge(s_xe, (e + 1) * NS)
                if s % QF == 0 and half == 0:
                    pe.wait_ge(s_w[k], (e * (NU // 2) + s // QF // 2 + 1) * 32)
                dst, full, lo, n = ((bankHA, s_upA, 0, CA), (bankHB, s_upB, CA, CB))[half]
                if not first:
                    pe.wait_ge((s_hA, s_hB)[half], j)
                kk = e % 2
                for c in range(DC):
                    rhs = xT[:, ds(kk, 1), c, lo:lo + n].rearrange("p k n -> p (k n)")
                    ins = pe.matmul(dst[:, 0:n], w1q[k][:, c, (s % QF) * P:(s % QF + 1) * P], rhs,
                                    start=(c == 0), stop=(c == DC - 1))
                ins.then_inc(full, 1)

            def down(e, s, half):
                j = e * NF + s
                k = (s // QF) % 2
                pe.wait_ge((s_hA, s_hB)[half], j + 1)
                src, tiles, used = ((hA, range(0, 3), s_dnA), (hB, range(3, NS), s_dnB))[half]
                for m, tile in enumerate(tiles):
                    ins = pe.matmul(bankY[:, tile, :], src[s % 2][:, m * P:(m + 1) * P], w2q[k][:, s % QF, :],
                                    start=False, stop=(s == NF - 1))
                ins.then_inc(used, 1)

            def expert(e, last):
                wait_apart(pe, s_b2, (e + 1) * 16)
                pe.wait_ge(s_yr, e * NS + 1)
                for tile in range(NS):
                    pe.matmul(bankY[:, tile, :], ones[0:1, :],
                              b2row[0:1, ds(e % 2, 1), :].rearrange("p k d -> p (k d)"), start=True, stop=False)
                for s in range(NF):
                    if s == NF // 2 and not last:
                        transposes(e + 1)
                    for half in (0, 1):
                        if s < NF - 1:
                            up(e, s + 1, half)
                        elif not last:
                            up(e + 1, 0, half)
                        down(e, s, half)

            transposes(0)
            up(0, 0, 0, True)
            up(0, 0, 1, True)
            with pe.Fori(0, E - 1) as e:
                expert(e, False)
            expert(E - 1, True)


_INS = ['x', 'ctx_1024', 'mask_BxS2_ik0', 'L0_xattn_Ws', 'L0_xattn_W', 'L0_xattn_w', 'L0_xattn_b', 'L0_xattn_Wcw',
        'L0_xattn_bcw', 'L0_xattn_Wcb', 'L0_xattn_bcb', 'L0_ffn_gate_w', 'L0_ffn_gate_b', 'L0_ffn_w1', 'L0_ffn_b1',
        'L0_ffn_w2', 'L0_ffn_b2']


def kernel(**inputs):
    import numpy as _np
    import concourse.bacc as _bacc
    from concourse import mybir as _mybir
    from concourse.bass_utils import run_bass_kernel_spmd as _run

    nc = _bacc.Bacc("TRN2", target_bir_lowering=False, num_devices=1)
    arrays, args = {}, []
    for name in _INS:
        a = _np.ascontiguousarray(inputs[name])
        arrays[f"in_{name}_dram"] = a
        args.append(nc.dram_tensor(f"in_{name}_dram", a.shape, _mybir.dt.from_np(a.dtype), kind="ExternalInput").ap())
    shape = inputs['x'].shape
    out = nc.dram_tensor("out_0_dram", shape, _mybir.dt.float32, kind="ExternalOutput").ap()
    xattn_moe_kernel(nc, *args, out)
    r = _run(nc, [arrays], core_ids=[0])
    return r.results[0]["out_0_dram"]
```

```python
import concourse.bass as bass
from concourse import mybir
from contextlib import ExitStack


def xattn_moe_kernel(nc, x, ctx, mask, Ws, W, w, b, Wcw, bcw, Wcb, bcb, gate_w, gate_b, w1, b1, w2, b2, out):
    fp32 = mybir.dt.float32
    i32 = mybir.dt.int32
    u32 = mybir.dt.uint32
    f32r = mybir.dt.float32r
    ALU = mybir.AluOpType
    ACT = mybir.ActivationFunctionType
    X = mybir.AxisListType.X
    ds = bass.ds

    P = 128
    B, S, D = x.shape
    T = ctx.shape[1]
    E, _, FF = w1.shape
    DC = D // P
    NI = S // P
    NF = FF // P
    TOK = B * S
    CAP = -(-5 * TOK // (4 * E))
    NS = CAP // P
    assert NS * P == CAP and NF % 8 == 0 and B % 2 == 0
    G = 4
    NG = -(-T // G)
    TP = NG * G
    HB_ = B // 2
    EPS = 1e-5
    NEG = 1e30
    BIG = 1.0e6
    MAGIC = 1597463007.0
    PAY = D + 4
    QF = 2
    NU = NF // QF
    NW = 4
    assert NU % 2 == 0 and NS == NW + 1 and NU >= 4

    buf = nc.dram_tensor("dispatched", (E * CAP, PAY), fp32, kind="Internal").ap()
    out_rows = out.rearrange("b s d -> (b s) d")

    st = ExitStack()
    with st:
        def sb(name, shape, dt=fp32):
            return st.enter_context(nc.sbuf_tensor(name, shape, dt))

        def sem(name):
            return st.enter_context(nc.semaphore(name))

        def phase():
            return st.enter_context(ExitStack())

        def part(stack, name, shape, dt=fp32):
            return stack.enter_context(nc.sbuf_tensor(name, shape, dt))[(slice(None),) * len(shape)]

        b1T = sb("b1T", [P, E * NF])
        tiles_ctl = sb("tiles_ctl", [1, E], i32)
        w1s = [sb(f"w1s{k}", [P, DC, QF * P]) for k in (0, 1)]
        w2s = [sb(f"w2s{k}", [P, QF, D]) for k in (0, 1)]
        slot_idx = [sb(f"slot_idx{k}", [P, NI], u32) for k in (0, 1)]
        ident = sb("ident", [P, P])
        triu = sb("triu", [P, P])
        ones = sb("ones", [P, P])
        onesel = sb("onesel", [P, G, G])
        wsel = sb("wsel", [P, G, G])
        w_col = sb("w_col", [P, DC])
        b_col = sb("b_col", [P, DC])
        wc_col = sb("wc_col", [P, 2, DC])
        bc_col = sb("bc_col", [P, 2])
        gwT = sb("gwT", [P, DC, E])
        gw_rows = sb("gw_rows", [E, D])
        gb_row = sb("gb_row", [P, E])
        mask_i = sb("mask_i", [T, B], i32)
        maskf = sb("maskf", [T, B])
        active = sb("active", [T, B])
        kpos = sb("kpos", [T, 4, B])
        t_index = sb("t_index", [P, 1])
        col_index = sb("col_index", [P, P])
        group_edge = sb("group_edge", [1, B, NG])
        past_edge = sb("past_edge", [1, B, NG])
        counts = sb("counts", [1, 4, B])
        ctl = sb("ctl", [1, 2, B], i32)
        erev = sb("erev", [P, E])
        ebase = sb("ebase", [P, E])
        tokid = sb("tokid", [P, NI])

        ln_st = sb("ln_st", [P, NI, 6])
        ln_mv = sb("ln_mv", [P, NI, 2])
        ln_v = sb("ln_v", [P, NI])
        ln_y = sb("ln_y", [P, NI], i32)
        ln_t = sb("ln_t", [P, 2, NI])
        mx = sb("mx", [P, NI])
        nd = sb("nd", [P, 3, NI])
        rden = sb("rden", [P, NI])
        ws_in = sb("ws_in", [P, 2, NI])
        ws = sb("ws", [P, 2, NI])
        lg = sb("lg", [P, NI, E])
        lgd = sb("lgd", [P, NI, E])
        lge = sb("lge", [P, NI, E])
        eq = sb("eq", [P, NI, E])
        onehot = sb("onehot", [P, NI, E])
        top = sb("top", [P, 2, NI])
        psum_e = sb("psum_e", [P, NI])
        run = sb("run", [P, NI + 1, E])
        cume = sb("cume", [P, 2, NI, E])
        pos = sb("pos", [P, 4, NI])
        out_idx = sb("out_idx", [P, NS], u32)
        load_n = sb("load_n", [1, 3, E])
        tile_edge = sb("tile_edge", [1, E, NS - 1])
        past_tile = sb("past_tile", [1, E, NS - 1])

        attention = phase()
        x_sb = [part(attention, f"x_sb{k}", [P, NI, D]) for k in (0, 1)]
        xn = [part(attention, f"xn{k}", [P, NI, D]) for k in (0, 1)]
        W_sb = part(attention, "W_sb", [P, DC, D])
        xnT = part(attention, "xnT", [P, DC, S])
        featT = part(attention, "featT", [P, DC, S])
        txtT = part(attention, "txtT", [P, DC, B, TP])
        bias_row = part(attention, "bias_row", [P, B, T])
        cw_row = part(attention, "cw_row", [P, B, T])
        cb_row = part(attention, "cb_row", [P, B, T])
        pay = [part(attention, f"pay{k}", [P, NI, PAY]) for k in (0, 1)]
        blank = part(attention, "blank", [P, PAY])

        prelude = phase()
        Ws_sb = part(prelude, "Ws_sb", [P, DC, D])
        ctx_sb = part(prelude, "ctx_sb", [T, B, D])
        perm = part(prelude, "perm", [T, B, T])
        wc_wide = part(prelude, "wc_wide", [P, 2, DC, P])
        ctxT = part(prelude, "ctxT", [P, DC, B, T])
        maskw = part(prelude, "maskw", [T, B, P])
        b1rows = part(prelude, "b1rows", [E * NF, P])
        prelude.close()

        h_ring = part(attention, "h_ring", [P, G, DC, S])
        partial = part(attention, "partial", [P, 2, S])
        rho_rows = part(attention, "rho_rows", [G, S])
        h2 = part(attention, "h2", [P, NI, D])
        h2T = part(attention, "h2T", [P, DC, S])
        z = part(attention, "z", [P, NI, T])
        zs = part(attention, "zs", [P, NI, T])
        prob = part(attention, "prob", [P, NI, T])
        pw = part(attention, "pw", [P, 2, NI, T])
        attention.close()

        experts = phase()
        xin = part(experts, "xin", [P, 2, NS, PAY])
        hx = [part(experts, f"hx{k}", [P, D]) for k in (0, 1)]
        y_out = part(experts, "y_out", [P, NS, D])
        b2wide = part(experts, "b2wide", [P, 2, D])
        relu_out = part(experts, "relu_out", [P, QF, CAP])
        xh = part(experts, "xh", [P, 2, DC, CAP], f32r)
        xl = part(experts, "xl", [P, 2, DC, CAP], f32r)
        w1h = [part(experts, f"w1h{k}", [P, DC, QF * P], f32r) for k in (0, 1)]
        w1l = [part(experts, f"w1l{k}", [P, DC, QF * P], f32r) for k in (0, 1)]
        w2h = [part(experts, f"w2h{k}", [P, QF, D], f32r) for k in (0, 1)]
        w2l = [part(experts, f"w2l{k}", [P, QF, D], f32r) for k in (0, 1)]
        hh = [part(experts, f"hh{k}", [P, QF, CAP], f32r) for k in (0, 1)]
        hl = [part(experts, f"hl{k}", [P, QF, CAP], f32r) for k in (0, 1)]

        PS = st.enter_context(nc.psum_tensor("PS", [P, 8, 512], fp32))
        bankA = [PS[:, 0, :], PS[:, 1, :]]
        bankR = PS[0:G, 2:4, :]
        bankT = PS[:, 4, :]
        bankL = PS[:, 5, :]
        bankY = PS[:, 0:NS, :]
        bankH = [PS[:, 5, :], PS[:, 6, :]]
        bankH4 = PS[:, 7, :]

        s_const = sem("const_built")
        s_ld = sem("keys_and_mask_loaded")
        s_ldw = sem("small_weights_loaded")
        s_ldW = sem("W_loaded")
        s_x = [sem(f"x_loaded_{k}") for k in (0, 1)]
        s_blank = sem("slots_blanked")
        s_pre = sem("prelude_dve_step")
        s_preA = sem("prelude_bank_filled")
        s_preF = sem("prelude_bank_read")
        s_preA2 = sem("attended_keys_counted")
        s_perm = sem("permutations_built")
        s_wide = sem("wide_columns_built")
        s_ctl = sem("group_counts_ready")
        s_ln = sem("ln_chain")
        s_xn = sem("xn_ready")
        s_afull = sem("bankA_filled")
        s_afree = sem("bankA_read")
        s_h = sem("tanh_ready")
        s_sum = sem("partial_ready")
        s_gch = sem("partial_chain")
        s_hfree = sem("rho_key_done")
        s_rfree = sem("bankR_read")
        s_row = sem("rho_group_transposed")
        s_ep = sem("epilogue_chain")
        s_zs = sem("scores_shifted")
        s_exp = sem("exp_done")
        s_wsin = sem("gates_in_ready")
        s_ws = sem("gates_ready")
        s_x2 = sem("x2_ready")
        s_h2 = sem("h2_ready")
        s_log = sem("logits_ready")
        s_lgd = sem("logits_shifted")
        s_lge = sem("logits_exp_done")
        s_oh = sem("onehot_ready")
        s_cnt = sem("expert_counts_ready")
        s_slot = sem("slots_ready")
        s_store = [sem(f"x2_stored_{k}") for k in (0, 1)]
        s_scat = sem("rows_dispatched")
        s_payfree = sem("payload_dispatched")
        s_yfree = sem("expert_buffer_written_out")
        s_w1 = [sem(f"w1_unit_loaded_{k}") for k in (0, 1)]
        s_w2 = [sem(f"w2_unit_loaded_{k}") for k in (0, 1)]
        s_w1h = sem("w1_high_parts_ready")
        s_w2h = sem("w2_high_parts_ready")
        s_w1l = sem("w1_split")
        s_w2l = sem("w2_split")
        s_b2 = sem("b2_loaded")
        s_xin = sem("expert_rows_loaded")
        s_fin = sem("tile_count_chain")
        s_tiles = sem("slot_tiles_counted")
        s_hx = sem("slot_tile_normalised")
        s_xf = sem("slot_tile_transposed")
        s_xh = sem("x_high_parts_ready")
        s_xl = sem("x_split")
        s_up = sem("hidden_in_psum")
        s_hf = sem("hidden_read")
        s_hh = sem("hidden_high_parts_ready")
        s_hl = sem("hidden_split")
        s_dn = sem("unit_added_to_output")
        s_u = sem("residual_rows_ready")
        s_yr = sem("expert_output_read")
        s_oidx = sem("token_numbers_ready")
        s_yo = sem("expert_rows_written")

        def z_half(rows, hf):
            return rows[:, hf * HB_:(hf + 1) * HB_, :].rearrange("p b t -> p (b t)")

        WIDE = NW * P
        HP = QF + 1
        FILLS = [s for p in range(NU // 2 - 1) for s in (p, p + 2)]
        assert sorted(set(FILLS)) == list(range(NS))
        PRE_FILLS = B + 2 + 4 + 2 * DC + 2
        EPI_STEPS = 39

        LN_STEPS = 13

        def wait_apart(engine, semaphore, value):
            value = value if isinstance(value, int) else engine.to_reg(value)
            engine.wait_ge(s_const, 1)
            engine.wait_ge(semaphore, value)

        block = st.enter_context(nc.Block())

        @block.sync
        def _(sp):
            sp.dma_start(mask_i[:, :], mask.rearrange("b t -> t b"), allow_slow_non_contiguous=True).then_inc(s_ld, 16)
            sp.dma_start(ctx_sb, ctx.rearrange("b t d -> t b d")).then_inc(s_ld, 16)
            for k in (0, 1):
                sp.dma_start(x_sb[k], x[k].rearrange("(i p) d -> p i d", p=P)).then_inc(s_x[k], 16)
            sp.dma_start(Ws_sb, Ws.rearrange("(c p) e -> p c e", p=P)).then_inc(s_ld, 16)
            sp.dma_start(W_sb[:, :, :], W.rearrange("(c p) e -> p c e", p=P)).then_inc(s_ldW, 16)

            def load_w1(e, i, k):
                sp.dma_start(w1s[k][:, :, :], w1[ds(e, 1), :, ds(i * QF * P, QF * P)]
                             .rearrange("e (c p) f -> p (e c) f", p=P)).then_inc(s_w1[k], 16)

            def load_w2(e, i, k):
                sp.dma_start(w2s[k][:, :, :], w2[ds(e, 1), ds(i * QF * P, QF * P), :]
                             .rearrange("e (g p) d -> p (e g) d", p=P)).then_inc(s_w2[k], 16)

            def batch(bb, k, last):
                sp.wait_ge(s_x2, bb + 1)
                if not last:
                    sp.dma_start(x_sb[k], x[bb + 2].rearrange("(i p) d -> p i d", p=P)).then_inc(s_x[k], 16)
                sp.dma_start(out[bb].rearrange("(i p) d -> p i d", p=P), pay[k][:, :, 0:D]).then_inc(s_store[k], 16)

            for k in (0, 1):
                load_w1(0, k, k)
                load_w2(0, k, k)
            with sp.Fori(0, HB_ - 1) as i:
                for k in (0, 1):
                    batch(2 * i + k, k, False)
            for k in (0, 1):
                batch(B - 2 + k, k, True)

            def load_rows(e):
                sp.dma_start(xin[:, ds(e % 2, 1), :, :].rearrange("p k s d -> p (k s) d"),
                             buf[ds(e * CAP, CAP), :].rearrange("(s p) d -> p s d", p=P)).then_inc(s_xin, 16)
                sp.dma_start(b2wide[:, ds(e % 2, 1), :].rearrange("p k d -> p (k d)"),
                             b2[ds(e, 1), :].broadcast_to([P, D])).then_inc(s_b2, 16)

            sp.wait_ge(s_slot, B)
            sp.wait_ge(s_scat, B * NI * 16)
            sp.wait_ge(s_tiles, 1)
            load_rows(0)

            def expert(e, last):
                def ahead(j, i, k, e_to, i_to, rows=False):
                    sp.wait_ge(s_w1l, j + 1)
                    load_w1(e_to, i_to, k)
                    if rows:
                        sp.wait_ge(s_yr, e * NS + 1)
                        load_rows(e + 1)
                    sp.wait_ge(s_w2l, j + 1)
                    load_w2(e_to, i_to, k)

                ahead(e * NU, 0, 0, e, 2)
                ahead(e * NU + 1, 1, 1, e, 3, rows=not last)
                with sp.Fori(0, NU // 2 - 2) as p:
                    for k in (0, 1):
                        ahead(e * NU + 2 * p + 2 + k, 2 * p + 2 + k, k, e, 2 * p + 4 + k)
                if not last:
                    for k in (0, 1):
                        ahead(e * NU + NU - 2 + k, NU - 2 + k, k, e + 1, k)

            with sp.Fori(0, E - 1) as e:
                expert(e, False)
            expert(E - 1, True)
            for k in (0, 1):
                sp.wait_ge(s_store[k], HB_ * 16 + 16)
            sp.wait_ge(s_yo, E * NS * 16)
            sp.wait_ge(s_blank, 16)

        @block.gpsimd
        def _(pool):
            pool.memset(ones[:, :], 1.0).then_inc(s_const, 1)
            pool.memset(ident[:, :], 0.0).then_inc(s_const, 1)
            pool.memset(blank[:, :], 0.0).then_inc(s_const, 1)
            pool.memset(onesel[:, :, :], 0.0).then_inc(s_const, 1)
            pool.memset(txtT[:, :, :, T:TP], 0.0).then_inc(s_const, 1)
            pool.memset(run[:, :, :], 0.0).then_inc(s_const, 1)
            pool.iota(col_index[:, :], pattern=[[1, P]], base=0, channel_multiplier=0,
                      allow_small_or_imprecise_dtypes=True).then_inc(s_const, 1)
            pool.iota(t_index[:, :], pattern=[[0, 1]], base=0, channel_multiplier=1,
                      allow_small_or_imprecise_dtypes=True).then_inc(s_const, 1)
            pool.iota(group_edge[:, :, :], pattern=[[0, B], [G, NG]], base=0, channel_multiplier=0,
                      allow_small_or_imprecise_dtypes=True).then_inc(s_const, 1)
            pool.iota(erev[:, :], pattern=[[-1, E]], base=E, channel_multiplier=0,
                      allow_small_or_imprecise_dtypes=True).then_inc(s_const, 1)
            pool.iota(ebase[:, :], pattern=[[CAP, E]], base=0, channel_multiplier=0,
                      allow_small_or_imprecise_dtypes=True).then_inc(s_const, 1)
            pool.iota(tile_edge[:, :, :], pattern=[[0, E], [P, NS - 1]], base=P, channel_multiplier=0,
                      allow_small_or_imprecise_dtypes=True).then_inc(s_const, 1)
            pool.iota(tokid[:, :], pattern=[[P, NI]], base=0, channel_multiplier=1,
                      allow_small_or_imprecise_dtypes=True).then_inc(s_const, 1)
            pool.wait_ge(s_const, 13)
            pool.affine_select(out=ident[:, :], in_=ident[:, :], compare_op=ALU.not_equal, fill=1.0,
                               base=0, pattern=[[-1, P]], channel_multiplier=1).then_inc(s_const, 1)
            pool.affine_select(out=triu[:, :], in_=ones[:, :], compare_op=ALU.is_ge, fill=0.0,
                               base=0, pattern=[[1, P]], channel_multiplier=-1).then_inc(s_const, 1)
            pool.affine_select(out=onesel[:, :, :], in_=onesel[:, :, :], compare_op=ALU.not_equal, fill=1.0,
                               base=0, pattern=[[1, G], [-1, G]], channel_multiplier=0).then_inc(s_const, 1)
            pool.memset(blank[:, PAY - 1:PAY], BIG).then_inc(s_const, 1)
            pool.wait_ge(s_const, 17)
            pool.dma_start(buf.rearrange("(s p) d -> p s d", p=P),
                           blank[:, None, :].broadcast_to([P, E * NS, PAY])).then_inc(s_blank, 16)
            pool.sem_inc(s_payfree, 2)
            for k in (0, 1):
                pool.sem_inc(s_store[k], 16)
            pool.sem_inc(s_yfree, 1)
            pool.wait_ge(s_blank, 16)

            def batch(bb, k):
                wait_apart(pool, s_slot, bb + 1)
                for i in range(NI):
                    pool.indirect_dma_start(buf, bass.IndirectOffsetOnAxis(ap=slot_idx[k][:, i:i + 1], axis=0),
                                            pay[k][:, i, :], None, bounds_check=E * CAP - 1,
                                            oob_is_err=False).then_inc(s_scat, 16)
                pool.wait_ge(s_scat, (bb + 1) * NI * 16)
                pool.sem_inc(s_payfree, 1)

            with pool.Fori(0, HB_) as i:
                for k in (0, 1):
                    batch(2 * i + k, k)

            for k in (0, 1):
                pool.wait_ge(s_store[k], HB_ * 16 + 16)
            with pool.Fori(0, E) as e:
                for s in range(NS):
                    wait_apart(pool, s_yr, e * NS + s + 2)
                    pool.indirect_dma_start(out_rows, bass.IndirectOffsetOnAxis(ap=out_idx[:, s:s + 1], axis=0),
                                            y_out[:, s, :], None, bounds_check=TOK - 1,
                                            oob_is_err=False).then_inc(s_yo, 16)
                pool.wait_ge(s_yo, (e + 1) * NS * 16)
                pool.sem_inc(s_yfree, 1)

        @block.scalar
        def _(act):
            act.dma_start(gw_rows[:, :], gate_w).then_inc(s_ldw, 16)
            act.dma_start(b1rows[:, :], b1.rearrange("e (f p) -> (e f) p", p=P)).then_inc(s_ldw, 16)
            act.dma_start(w_col[:, :], w.rearrange("(c p) o -> p (c o)", p=P),
                          allow_slow_non_contiguous=True).then_inc(s_ldw, 16)
            act.dma_start(b_col[:, :], b.rearrange("o (c p) -> p (o c)", p=P),
                          allow_slow_non_contiguous=True).then_inc(s_ldw, 16)
            act.dma_start(wc_col[:, 0, :], Wcw.rearrange("o (c p) -> p (o c)", p=P),
                          allow_slow_non_contiguous=True).then_inc(s_ldw, 16)
            act.dma_start(wc_col[:, 1, :], Wcb.rearrange("o (c p) -> p (o c)", p=P),
                          allow_slow_non_contiguous=True).then_inc(s_ldw, 16)
            act.dma_start(bc_col[:, 0:1], bcw.rearrange("(a o) -> a o", a=1).broadcast_to([P, 1])).then_inc(s_ldw, 16)
            act.dma_start(bc_col[:, 1:2], bcb.rearrange("(a o) -> a o", a=1).broadcast_to([P, 1])).then_inc(s_ldw, 16)
            act.dma_start(gb_row[:, :], gate_b.rearrange("(a o) -> a o", a=1).broadcast_to([P, E])).then_inc(s_ldw, 16)

            f = 0

            def filled():
                nonlocal f
                f += 1
                act.wait_ge(s_preA, f)

            for n in range(B):
                filled()
                act.activation(ctxT[:, :, n, :], bankA[(f - 1) % 2][:, 0:DC * T].rearrange("p (c t) -> p c t", c=DC),
                               ACT.Copy).then_inc(s_preF, 1)
            for hf in (0, 1):
                filled()
                act.activation(z_half(bias_row, hf), bankA[(f - 1) % 2][:, 0:HB_ * T], ACT.Copy).then_inc(s_preF, 1)
            for which in (cw_row, cb_row):
                for hf in (0, 1):
                    filled()
                    act.activation(z_half(which, hf), bankA[(f - 1) % 2][:, 0:HB_ * T], ACT.Copy).then_inc(s_preF, 1)
            act.wait_ge(s_ldw, 9 * 16)
            for c in range(DC):
                for hf in (0, 1):
                    filled()
                    act.activation(txtT[:, c, hf * HB_:(hf + 1) * HB_, 0:T],
                                   bankA[(f - 1) % 2][:, 0:HB_ * T].rearrange("p (b t) -> p b t", b=HB_),
                                   ACT.Identity, bias=b_col[:, c:c + 1]).then_inc(s_preF, 1)
            filled()
            act.activation(gwT[:, :, :], bankA[(f - 1) % 2][:, 0:DC * E].rearrange("p (c e) -> p c e", c=DC),
                           ACT.Copy).then_inc(s_preF, 1)
            filled()
            act.activation(b1T[:, :], bankA[(f - 1) % 2][:, 0:E * NF], ACT.Copy).then_inc(s_preF, 1)
            assert f == PRE_FILLS

            def feat_evacs(base):
                for c in range(DC):
                    act.wait_ge(s_afull, base + c + 1)
                    act.activation(xnT[:, c, :], bankA[c % 2], ACT.Copy).then_inc(s_afree, 1)

            def proj_evacs(base):
                for c in range(DC):
                    act.wait_ge(s_afull, base + DC + c + 1)
                    act.activation(featT[:, c, :], bankA[c % 2], ACT.Copy).then_inc(s_afree, 1)

            feat_evacs(0)
            proj_evacs(0)
            act.wait_ge(s_afree, 2 * DC)
            act.wait_ge(s_preF, PRE_FILLS)
            act.wait_ge(s_ctl, 1)

            def batch(bb, last):
                n = act.value_load(ctl[0:1, 0, ds(bb, 1)], min_val=1, max_val=NG)
                k0 = act.value_load(ctl[0:1, 1, ds(bb, 1)], min_val=0, max_val=B * NG)
                with act.Fori(0, n) as g:
                    for t in range(G):
                        wait_apart(act, s_hfree, (k0 + g) * G + t + 1)
                        for c in range(DC):
                            ins = act.activation(h_ring[:, t, c, :], featT[:, c, :], ACT.Tanh,
                                                 bias=txtT[:, c, ds(bb, 1), ds(g * G + t, 1)].rearrange("p b t -> p (b t)"))
                        ins.then_inc(s_h, 1)
                base = 2 * DC + bb * 3 * DC
                if not last:
                    feat_evacs(base)
                act.wait_ge(s_zs, bb + 1)
                act.activation(prob[:, :, :], zs[:, :, :], ACT.Exp).then_inc(s_exp, 1)
                act.wait_ge(s_wsin, bb + 1)
                for m in (0, 1):
                    act.activation(ws[:, m, :], ws_in[:, m, :], ACT.Tanh, bias=bc_col[:, m:m + 1]).then_inc(s_ws, 1)
                if not last:
                    proj_evacs(base)
                    base = base + 2 * DC
                for c in range(DC):
                    act.wait_ge(s_afull, base + c + 1)
                    act.activation(h2T[:, c, :], bankA[c % 2], ACT.Copy).then_inc(s_afree, 1)
                act.wait_ge(s_lgd, bb + 1)
                act.activation(lge[:, :, :], lgd[:, :, :], ACT.Exp).then_inc(s_lge, 1)
                if not last:
                    act.wait_ge(s_afree, base + DC)

            with act.Fori(0, B - 1) as bb:
                batch(bb, False)
            batch(B - 1, True)

            act.wait_ge(s_tiles, 1)

            def w1_high(j, k, n):
                act.wait_ge(s_w1[k], (n + 1) * 16)
                act.wait_ge(s_up, HP * j + HP)
                act.activation(w1h[k][:, :, :], w1s[k][:, :, :], ACT.Copy).then_inc(s_w1h, 1)

            def w2_high(j, k, n):
                act.wait_ge(s_w2[k], (n + 1) * 16)
                act.wait_ge(s_dn, j + 1)
                act.activation(w2h[k][:, :, :], w2s[k][:, :, :], ACT.Copy).then_inc(s_w2h, 1)

            def hidden(j):
                for m in range(HP):
                    act.wait_ge(s_hl, HP * j + m + 1)
                    wait_apart(act, s_up, HP * (j + 2) + m + 1)
                    for f in ([m] if m < QF else range(QF)):
                        src, cols = (bankH[f], slice(0, WIDE)) if m < QF else                             (bankH4[:, f * P:(f + 1) * P], slice(WIDE, CAP))
                        ins = act.activation(relu_out[:, f, cols], src, ACT.Relu, bias=b1T[:, ds(j * QF + f, 1)])
                    ins.then_inc(s_hf, 1)

            def x_high(fill, e, s, bank):
                act.wait_ge(s_xf, fill + 1)
                act.activation(xh[:, ds(e % 2, 1), :, ds(s * P, P)].rearrange("p k c n -> p (k c) n"),
                               bankH[bank].rearrange("p (c n) -> p c n", c=DC), ACT.Copy).then_inc(s_xh, 1)

            for n, s in enumerate(FILLS):
                x_high(n, 0, s, n % 2)
            w1_high(0, 0, 0)

            def first_turn(e):
                w1_high(e * NU + 1, 1, e * (NU // 2))
                hidden(e * NU)
                w2_high(e * NU, 0, e * (NU // 2))

            def expert(e, last):
                w1_high(e * NU + 2, 0, e * (NU // 2) + 1)
                hidden(e * NU + 1)
                w2_high(e * NU + 1, 1, e * (NU // 2))
                with act.Fori(0, NU // 2 - 2) as p:
                    j = e * NU + 2 * p + 2
                    n = e * (NU // 2) + p + 1
                    fill = (e + 1) * len(FILLS) + 2 * p
                    w1_high(j + 1, 1, n)
                    hidden(j)
                    if not last:
                        x_high(fill, e + 1, p, 0)
                    w2_high(j, 0, n)
                    if not last:
                        x_high(fill + 1, e + 1, p + 2, 1)
                    w1_high(j + 2, 0, n + 1)
                    hidden(j + 1)
                    w2_high(j + 1, 1, n)
                j = e * NU + NU - 2
                n = (e + 1) * (NU // 2) - 1
                fill = (e + 2) * len(FILLS) - 2
                w1_high(j + 1, 1, n)
                hidden(j)
                if not last:
                    x_high(fill, e + 1, NU // 2 - 2, 0)
                w2_high(j, 0, n)
                if not last:
                    x_high(fill + 1, e + 1, NU // 2, 1)
                    w1_high(j + 2, 0, n + 1)
                hidden(j + 1)
                w2_high(j + 1, 1, n)
                if not last:
                    first_turn(e + 1)

            first_turn(0)
            with act.Fori(0, E - 1) as e:
                expert(e, False)
            expert(E - 1, True)

        @block.vector
        def _(dve):
            def wait(engine, semaphore, value):
                engine.wait_ge(semaphore, value)

            class Chain:

                def __init__(self, semaphore, base):
                    self.semaphore, self.base, self.n = semaphore, base, 0

                def link(self, ins, apart=False):
                    self.n += 1
                    ins.then_inc(self.semaphore, 1)
                    (wait_apart if apart else wait)(dve, self.semaphore, self.base + self.n)

            dve.sem_inc(s_rfree, 2)
            dve.sem_inc(s_hfree, G)
            dve.sem_inc(s_yr, 1)
            dve.sem_inc(s_up, 2 * HP)
            dve.sem_inc(s_hf, HP)
            dve.sem_inc(s_hl, HP)
            dve.sem_inc(s_dn, 2)

            pre = Chain(s_pre, 0)
            dve.wait_ge(s_ld, 3 * 16)
            dve.wait_ge(s_const, 17)
            pre.link(dve.tensor_copy(maskf[:, :], mask_i[:, :]))
            pre.link(dve.tensor_scalar(active[:, :], maskf[:, :], 0.0, None, ALU.is_gt))
            dve.wait_ge(s_preA2, 1)
            cnt_cum, cnt_all = bankT[0:T, 0:B], bankT[:, B:2 * B]
            pre.link(dve.tensor_copy(kpos[:, 3, :], cnt_cum))
            pre.link(dve.scalar_tensor_tensor(kpos[:, 0, :], bankT[0:T, B:2 * B], t_index[0:T, 0:1], kpos[:, 3, :],
                                              ALU.add, ALU.subtract))
            pre.link(dve.scalar_tensor_tensor(kpos[:, 1, :], kpos[:, 3, :], -1.0, kpos[:, 0, :],
                                              ALU.add, ALU.subtract))
            pre.link(dve.tensor_tensor(kpos[:, 2, :], kpos[:, 1, :], active[:, :], ALU.mult))
            pre.link(dve.tensor_tensor(kpos[:, 3, :], kpos[:, 2, :], kpos[:, 0, :], ALU.add))
            for n in range(B):
                dve.tensor_scalar(maskw[:, n, :], ones[0:T, :], maskf[:, n:n + 1], None, ALU.mult)
                ins = dve.tensor_scalar(perm[:, n, :], col_index[0:T, 0:T], kpos[:, 3, n:n + 1], None, ALU.is_equal)
            ins.then_inc(s_perm, 1)
            pre.link(dve.tensor_copy(counts[:, 0, :], bankT[0:1, B:2 * B]))
            pre.link(dve.tensor_tensor(past_edge[:, :, :], counts[:, 0, :][:, :, None].broadcast_to([1, B, NG]),
                                       group_edge[:, :, :], ALU.is_gt))
            pre.link(dve.tensor_reduce(counts[:, 1, :], past_edge[:, :, :], X, ALU.add))
            pre.link(dve.tensor_scalar(counts[:, 1, :], counts[:, 1, :], 1.0, None, ALU.max))
            pre.link(dve.tensor_tensor_scan(counts[:, 2, :], ones[0:1, 0:B], counts[:, 1, :], 0.0,
                                            ALU.mult, ALU.add))
            pre.link(dve.tensor_tensor(counts[:, 3, :], counts[:, 2, :], counts[:, 1, :], ALU.subtract))
            pre.link(dve.tensor_copy(ctl[:, 0, :], counts[:, 1, :]))
            pre.link(dve.tensor_copy(ctl[:, 1, :], counts[:, 3, :]))
            dve.nop().then_inc(s_ctl, 1)
            pre.link(dve.memset(bankT, 0.0))
            dve.wait_ge(s_ldw, 9 * 16)
            for m in (0, 1):
                for c in range(DC):
                    dve.tensor_scalar(wc_wide[:, m, c, :], ones[:, :], wc_col[:, m, c:c + 1], None, ALU.mult)
            dve.tensor_scalar(wsel[:, :, :], onesel[:, :, :], w_col[:, 0:1], None, ALU.mult).then_inc(s_wide, 1)

            def rsqrt(chain, var):
                y = ln_y[:, :].bitcast(fp32)
                chain.link(dve.tensor_scalar(ln_v[:, :], var, EPS, None, ALU.add))
                chain.link(dve.tensor_scalar(ln_y[:, :], ln_v[:, :].bitcast(i32), -0.5, MAGIC, ALU.mult, ALU.add))
                for _ in range(3):
                    chain.link(dve.tensor_tensor(ln_t[:, 0, :], y, y, ALU.mult))
                    chain.link(dve.scalar_tensor_tensor(ln_t[:, 1, :], ln_t[:, 0, :], -0.5, ln_v[:, :],
                                                        ALU.mult, ALU.mult))
                    chain.link(dve.scalar_tensor_tensor(y, ln_t[:, 1, :], 1.5, y, ALU.add, ALU.mult))
                return y

            def moments(chain, src):
                for i in range(NI - 1):
                    dve.bn_stats(ln_st[:, i, :], src(i))
                chain.link(dve.bn_stats(ln_st[:, NI - 1, :], src(NI - 1)), True)
                for i in range(NI - 1):
                    dve.bn_aggr(ln_mv[:, i, :], ln_st[:, i, :])
                chain.link(dve.bn_aggr(ln_mv[:, NI - 1, :], ln_st[:, NI - 1, :]))

            def ln1(ib, k):
                chain = Chain(s_ln, (2 * ib + k) * LN_STEPS)
                dve.wait_ge(s_x[k], (ib + 1) * 16)
                moments(chain, lambda i: x_sb[k][:, i, :])
                y = rsqrt(chain, ln_mv[:, :, 1])
                for i in range(NI):
                    ins = dve.tensor_scalar(xn[k][:, i, :], x_sb[k][:, i, :], ln_mv[:, i, 0:1], y[:, i:i + 1],
                                            ALU.subtract, ALU.mult)
                ins.then_inc(s_xn, 1)
                assert chain.n == LN_STEPS

            ln1(0, 0)
            ln1(0, 1)
            dve.wait_ge(s_preF, B + 2)
            pre.link(dve.tensor_scalar(bias_row[:, :, :], bias_row[:, :, :], -1.0, NEG, ALU.add, ALU.mult))
            dve.wait_ge(s_preF, B + 6)

            def groups(bb):
                n = dve.value_load(ctl[0:1, 0, ds(bb, 1)], min_val=1, max_val=NG)
                k0 = dve.value_load(ctl[0:1, 1, ds(bb, 1)], min_val=0, max_val=B * NG)
                with dve.Fori(0, n) as g:
                    kk = k0 + g
                    for t in range(G):
                        dve.wait_ge(s_h, kk * G + t + 1)
                        dve.wait_ge(s_hfree, kk * G + t + 3)
                        chain = Chain(s_gch, kk * 2 * G + 2 * t)
                        part = partial[:, t % 2, :]
                        chain.link(dve.tensor_scalar(part, h_ring[:, t, 1, :], w_col[:, 1:2], None, ALU.mult))
                        chain.link(dve.scalar_tensor_tensor(part, h_ring[:, t, 2, :], w_col[:, 2:3], part,
                                                            ALU.mult, ALU.add))
                        dve.scalar_tensor_tensor(part, h_ring[:, t, 3, :], w_col[:, 3:4], part,
                                                 ALU.mult, ALU.add).then_inc(s_sum, 1)
                    dve.wait_ge(s_hfree, kk * G + G + G)
                    dve.wait_ge(s_row, kk + 1)
                    dve.tensor_copy(rho_rows[:, :], bankR[:, ds(kk % 2, 1), :].rearrange("p a f -> p (a f)"))\
                       .then_inc(s_rfree, 1)
                dve.wait_ge(s_row, k0 + n + 1)

            def epilogue(ib, k, last):
                bb = 2 * ib + k
                ep = Chain(s_ep, bb * EPI_STEPS)
                rT = bankT.rearrange("p (i t) -> p i t", i=NI)[:, :, 0:T]

                def key_row(r):
                    return r[:, ds(bb, 1), :].broadcast_to([P, NI, T])

                ep.link(dve.tensor_tensor(z[:, :, :], rT, key_row(bias_row), ALU.add))
                ep.link(dve.tensor_reduce(mx[:, :], z[:, :, :], X, ALU.max))
                dve.tensor_tensor(zs[:, :, :], z[:, :, :], mx[:, :][:, :, None].broadcast_to([P, NI, T]),
                                  ALU.subtract).then_inc(s_zs, 1)
                dve.wait_ge(s_exp, bb + 1)
                dve.tensor_reduce(nd[:, 0, :], prob[:, :, :], X, ALU.add)
                ep.link(dve.tensor_tensor(pw[:, 0, :, :], prob[:, :, :], key_row(cw_row), ALU.mult))
                ep.link(dve.tensor_tensor(pw[:, 1, :, :], prob[:, :, :], key_row(cb_row), ALU.mult))
                dve.reciprocal(rden[:, :], nd[:, 0, :])
                ep.link(dve.tensor_reduce(nd[:, 1:3, :], pw[:, :, :, :], X, ALU.add))
                dve.tensor_tensor(ws_in[:, :, :], nd[:, 1:3, :], rden[:, None, :].broadcast_to([P, 2, NI]),
                                  ALU.mult).then_inc(s_wsin, 1)
                dve.wait_ge(s_payfree, bb + 1)
                dve.wait_ge(s_store[k], ib * 16 + 16)
                dve.wait_ge(s_ws, 2 * bb + 2)
                for i in range(NI):
                    ins = dve.tensor_scalar(pay[k][:, i, 0:D], xn[k][:, i, :], ws[:, 0, i:i + 1], ws[:, 1, i:i + 1],
                                            ALU.mult, ALU.add)
                ep.link(ins)
                for i in range(NI):
                    ins = dve.tensor_tensor(pay[k][:, i, 0:D], pay[k][:, i, 0:D], x_sb[k][:, i, :], ALU.add)
                ep.link(ins)
                dve.nop().then_inc(s_x2, 1)
                moments(ep, lambda i: pay[k][:, i, 0:D])
                y = rsqrt(ep, ln_mv[:, :, 1])
                for i in range(NI):
                    ins = dve.tensor_scalar(h2[:, i, :], pay[k][:, i, 0:D], ln_mv[:, i, 0:1], y[:, i:i + 1],
                                            ALU.subtract, ALU.mult)
                ins.then_inc(s_h2, 1)
                dve.tensor_copy(pay[k][:, :, D], ln_mv[:, :, 0])
                dve.tensor_copy(pay[k][:, :, D + 1], y)
                dve.tensor_copy(pay[k][:, :, D + 3], tokid[:, :])
                ep.link(dve.tensor_scalar(pos[:, 3, :], tokid[:, :], float(S), None, ALU.add))
                ep.link(dve.tensor_copy(tokid[:, :], pos[:, 3, :]))
                if not last:
                    ln1(ib + 1, k)
                dve.wait_ge(s_log, bb + 1)
                ep.link(dve.tensor_tensor(lg[:, :, :], bankL[:, 0:NI * E].rearrange("p (i e) -> p i e", i=NI),
                                          gb_row[:, None, :].broadcast_to([P, NI, E]), ALU.add))
                ep.link(dve.tensor_reduce(top[:, 0, :], lg[:, :, :], X, ALU.max))
                top_wide = top[:, 0, :][:, :, None].broadcast_to([P, NI, E])
                dve.tensor_tensor(lgd[:, :, :], lg[:, :, :], top_wide, ALU.subtract).then_inc(s_lgd, 1)
                ep.link(dve.tensor_tensor(eq[:, :, :], lg[:, :, :], top_wide, ALU.is_equal))
                ep.link(dve.tensor_tensor(eq[:, :, :], eq[:, :, :], erev[:, None, :].broadcast_to([P, NI, E]), ALU.mult))
                ep.link(dve.tensor_reduce(top[:, 1, :], eq[:, :, :], X, ALU.max))
                dve.tensor_tensor(onehot[:, :, :], eq[:, :, :], top[:, 1, :][:, :, None].broadcast_to([P, NI, E]),
                                  ALU.is_equal).then_inc(s_oh, 1)
                dve.wait_ge(s_lge, bb + 1)
                ep.link(dve.tensor_reduce(psum_e[:, :], lge[:, :, :], X, ALU.add))
                dve.reciprocal(pay[k][:, :, D + 2], psum_e[:, :])
                dve.wait_ge(s_cnt, bb + 1)
                cnt = bankL[:, 64:64 + NI * E].rearrange("p (i e) -> p i e", i=NI)
                tot = bankL[:, 128:128 + NI * E].rearrange("p (i e) -> p i e", i=NI)
                ep.link(dve.tensor_copy(run[:, 0, :], run[:, NI, :]))
                for i in range(NI):
                    ep.link(dve.tensor_tensor(run[:, i + 1, :], run[:, i, :], tot[:, i, :], ALU.add))
                ep.link(dve.tensor_tensor(cume[:, 0, :, :], cnt, run[:, 0:NI, :], ALU.add))
                ep.link(dve.tensor_tensor(cume[:, 0, :, :], cume[:, 0, :, :], onehot[:, :, :], ALU.mult))
                ep.link(dve.tensor_tensor(cume[:, 1, :, :], onehot[:, :, :],
                                          ebase[:, None, :].broadcast_to([P, NI, E]), ALU.mult))
                ep.link(dve.tensor_reduce(pos[:, 0:2, :], cume[:, :, :, :], X, ALU.add))
                ep.link(dve.tensor_scalar(pos[:, 2, :], pos[:, 0, :], float(CAP), BIG, ALU.is_gt, ALU.mult))
                ep.link(dve.scalar_tensor_tensor(pos[:, 3, :], pos[:, 0, :], -1.0, pos[:, 1, :], ALU.add, ALU.add))
                dve.tensor_tensor(slot_idx[k][:, :], pos[:, 3, :], pos[:, 2, :], ALU.add).then_inc(s_slot, 1)
                assert ep.n == EPI_STEPS, ep.n

            dve.sem_inc(s_row, 1)
            with dve.Fori(0, HB_ - 1) as i:
                for k in (0, 1):
                    groups(2 * i + k)
                    epilogue(i, k, False)
            for k in (0, 1):
                groups(B - 2 + k)
                epilogue(HB_ - 1, k, True)

            fin = Chain(s_fin, 0)
            fin.link(dve.tensor_copy(load_n[:, 0, :], run[0:1, NI, :]))
            fin.link(dve.tensor_tensor(past_tile[:, :, :], load_n[:, 0, :][:, :, None].broadcast_to([1, E, NS - 1]),
                                       tile_edge[:, :, :], ALU.is_gt))
            fin.link(dve.tensor_reduce(load_n[:, 1, :], past_tile[:, :, :], X, ALU.add))
            fin.link(dve.tensor_scalar(tiles_ctl[:, :], load_n[:, 1, :], 1.0, None, ALU.add))
            fin.link(dve.memset(PS[:, :, :], 0.0))
            dve.sem_inc(s_tiles, 1)

            def rows_of(e):
                return xin[:, ds(e % 2, 1), :, :].rearrange("p k s d -> p (k s) d")

            def w1_low(j, k):
                dve.wait_ge(s_w1h, j + 1)
                dve.tensor_tensor(w1l[k][:, :, :], w1s[k][:, :, :], w1h[k][:, :, :].bitcast(fp32), ALU.subtract)\
                   .then_inc(s_w1l, 1)

            def w2_low(j, k):
                dve.wait_ge(s_w2h, j + 1)
                dve.tensor_tensor(w2l[k][:, :, :], w2s[k][:, :, :], w2h[k][:, :, :].bitcast(fp32), ALU.subtract)\
                   .then_inc(s_w2l, 1)

            def hidden(j, k):
                for m in range(HP):
                    part_of = (slice(None), m, slice(0, WIDE)) if m < QF else (slice(None), slice(None), slice(WIDE, CAP))
                    src, high, low = relu_out[part_of], hh[k][part_of], hl[k][part_of]
                    dve.wait_ge(s_dn, j + 1)
                    dve.wait_ge(s_hf, HP * (j + 1) + m + 1)
                    dve.tensor_copy(high, src).then_inc(s_hh, 1)
                    dve.wait_ge(s_hh, HP * j + m + 1)
                    dve.tensor_tensor(low, src, high.bitcast(fp32), ALU.subtract).then_inc(s_hl, 1)

            def x_rows(fill, e, s, b):
                dve.wait_ge(s_xin, (e + 1) * 16)
                if fill is not None:
                    dve.wait_ge(s_xf, fill - 1)
                rows = rows_of(e)
                tile = lambda a, z: rows[:, ds(s, 1), a:z].rearrange("p s d -> p (s d)")
                dve.tensor_scalar(hx[b][:, :], tile(0, D), tile(D, D + 1), tile(D + 1, D + 2),
                                  ALU.subtract, ALU.mult).then_inc(s_hx, 1)

            def x_low(fill, e, s, bank):
                dve.wait_ge(s_xh, fill + 1)
                cols = [q[:, ds(e % 2, 1), :, ds(s * P, P)].rearrange("p k c n -> p (k c) n") for q in (xh, xl)]
                dve.tensor_tensor(cols[1], bankH[bank].rearrange("p (c n) -> p c n", c=DC), cols[0].bitcast(fp32),
                                  ALU.subtract).then_inc(s_xl, 1)

            def residual(e):
                dve.wait_ge(s_b2, (e + 1) * 16)
                dve.wait_ge(s_yfree, e + 1)
                rows = rows_of(e)
                b2e = b2wide[:, ds(e % 2, 1), :].rearrange("p k d -> p (k d)")
                for s in range(NS):
                    dve.scalar_tensor_tensor(y_out[:, s, :], b2e, rows[:, s, D + 2:D + 3], rows[:, s, 0:D],
                                             ALU.mult, ALU.add)
                dve.tensor_copy(out_idx[:, :], rows[:, :, D + 3]).then_inc(s_u, 1)

            def finish(e):
                rows = rows_of(e)
                dve.wait_ge(s_u, e + 1)
                dve.wait_ge(s_dn, (e + 1) * NU + 2)
                for s in range(NS):
                    dve.scalar_tensor_tensor(y_out[:, s, :], bankY[:, s, :], rows[:, s, D + 2:D + 3], y_out[:, s, :],
                                             ALU.mult, ALU.add).then_inc(s_yr, 1)

            def first_turn(e):
                w1_low(e * NU + 1, 1)
                hidden(e * NU, 0)
                w2_low(e * NU, 0)

            def expert(e, last):
                def pair(j, fill, p, tail):
                    w1_low(j + 1, 1)
                    if not last:
                        x_rows(fill, e + 1, p, 0)
                        x_rows(fill + 1, e + 1, p + 2, 1)
                    hidden(j, 0)
                    if not last:
                        x_low(fill, e + 1, p, 0)
                    w2_low(j, 0)
                    if not last:
                        x_low(fill + 1, e + 1, p + 2, 1)
                    if not (last and tail):
                        w1_low(j + 2, 0)
                    hidden(j + 1, 1)
                    w2_low(j + 1, 1)

                w1_low(e * NU + 2, 0)
                hidden(e * NU + 1, 1)
                w2_low(e * NU + 1, 1)
                with dve.Fori(0, NU // 2 - 2) as p:
                    pair(e * NU + 2 * p + 2, (e + 1) * len(FILLS) + 2 * p, p, False)
                pair(e * NU + NU - 2, (e + 2) * len(FILLS) - 2, NU // 2 - 2, True)
                residual(e)
                if not last:
                    first_turn(e + 1)
                finish(e)

            for n, s in enumerate(FILLS):
                x_rows(n if n > 1 else None, 0, s, n % 2)
                x_low(n, 0, s, n % 2)
            w1_low(0, 0)
            first_turn(0)
            with dve.Fori(0, E - 1) as e:
                expert(e, False)
            expert(E - 1, True)

        @block.tensor
        def _(pe):
            pe.wait_ge(s_const, 17)
            pe.wait_ge(s_pre, 2)
            pe.matmul(bankT[0:T, 0:B], triu[0:T, 0:T], active[:, :], start=True, stop=True)
            pe.matmul(bankT[:, B:2 * B], ones[0:T, :], active[:, :], start=True, stop=True).then_inc(s_preA2, 1)
            pe.wait_ge(s_ld, 3 * 16)
            pe.wait_ge(s_perm, 1)
            f = 0

            def bank():
                nonlocal f
                f += 1
                if f > 2:
                    pe.wait_ge(s_preF, f - 2)
                return bankA[(f - 1) % 2]

            for n in range(B):
                bk = bank()
                for c in range(DC):
                    ins = pe.matmul(bk[:, c * T:(c + 1) * T], ctx_sb[:, n, c * P:(c + 1) * P], perm[:, n, :],
                                    start=True, stop=True)
                ins.then_inc(s_preA, 1)
            for hf in (0, 1):
                bk = bank()
                for n in range(HB_):
                    ins = pe.matmul(bk[:, n * T:(n + 1) * T], maskw[:, hf * HB_ + n, :], perm[:, hf * HB_ + n, :],
                                    start=True, stop=True)
                ins.then_inc(s_preA, 1)

            def keys(c, hf):
                return ctxT[:, c, hf * HB_:(hf + 1) * HB_, :].rearrange("p b t -> p (b t)")

            pe.wait_ge(s_wide, 1)
            pe.wait_ge(s_preF, B)
            for m in (0, 1):
                for hf in (0, 1):
                    bk = bank()
                    for c in range(DC):
                        ins = pe.matmul(bk[:, 0:HB_ * T], wc_wide[:, m, c, :], keys(c, hf),
                                        start=(c == 0), stop=(c == DC - 1))
                    ins.then_inc(s_preA, 1)
            for c2 in range(DC):
                for hf in (0, 1):
                    bk = bank()
                    for c in range(DC):
                        ins = pe.matmul(bk[:, 0:HB_ * T], Ws_sb[:, c, c2 * P:(c2 + 1) * P], keys(c, hf),
                                        start=(c == 0), stop=(c == DC - 1))
                    ins.then_inc(s_preA, 1)
            bk = bank()
            pe.wait_ge(s_ldw, 9 * 16)
            for c in range(DC):
                ins = pe.transpose(bk[:, c * E:(c + 1) * E], gw_rows[:, c * P:(c + 1) * P], ident[0:E, 0:E])
            ins.then_inc(s_preA, 1)
            bk = bank()
            pe.transpose(bk[:, 0:E * NF], b1rows[:, :], ident[:, :]).then_inc(s_preA, 1)
            assert f == PRE_FILLS
            pe.wait_ge(s_preF, PRE_FILLS)

            def take(u, first=False):
                if not first:
                    pe.wait_ge(s_afree, u - 1)

            def features(base, k, bb, first):
                pe.wait_ge(s_xn, bb + 1)
                for c in range(DC):
                    take(base + c, first and c < 2)
                    for i in range(NI):
                        ins = pe.transpose(bankA[c % 2][:, i * P:(i + 1) * P], xn[k][:, i, c * P:(c + 1) * P], ident[:, :])
                    ins.then_inc(s_afull, 1)
                for c2 in range(DC):
                    take(base + DC + c2)
                    for c in range(DC):
                        if c2 == 0:
                            pe.wait_ge(s_afree, base + c + 1)
                        ins = pe.matmul(bankA[c2 % 2], W_sb[:, c, c2 * P:(c2 + 1) * P], xnT[:, c, :],
                                        start=(c == 0), stop=(c == DC - 1))
                    ins.then_inc(s_afull, 1)

            pe.wait_ge(s_ldW, 16)
            features(0, 0, 0, True)
            pe.wait_ge(s_ctl, 1)

            def batch(bb, k, last):
                n = pe.value_load(ctl[0:1, 0, ds(bb, 1)], min_val=1, max_val=NG)
                k0 = pe.value_load(ctl[0:1, 1, ds(bb, 1)], min_val=0, max_val=B * NG)
                with pe.Fori(0, n) as g:
                    kk = k0 + g
                    pe.wait_ge(s_rfree, kk + 1)
                    bk = bankR[:, ds(kk % 2, 1), :].rearrange("p a f -> p (a f)")
                    for t in range(G):
                        wait_apart(pe, s_h, kk * G + t + 1)
                        pe.matmul(bk, wsel[:, t, :], h_ring[:, t, 0, :], start=(t == 0), stop=False)
                        wait_apart(pe, s_sum, kk * G + t + 1)
                        pe.matmul(bk, onesel[:, t, :], partial[:, t % 2, :], start=False,
                                  stop=(t == G - 1)).then_inc(s_hfree, 1)
                    wait_apart(pe, s_rfree, kk + 3)
                    for i in range(NI):
                        ins = pe.matmul(bankT[:, ds(g * G + i * P, G)], rho_rows[:, i * P:(i + 1) * P],
                                        ident[0:G, 0:G], start=True, stop=True)
                    ins.then_inc(s_row, 1)
                base = 2 * DC + bb * 3 * DC
                if not last:
                    features(base, 1 - k, bb + 1, False)
                    base = base + 2 * DC
                pe.wait_ge(s_h2, bb + 1)
                for c in range(DC):
                    take(base + c)
                    for i in range(NI):
                        ins = pe.transpose(bankA[c % 2][:, i * P:(i + 1) * P], h2[:, i, c * P:(c + 1) * P], ident[:, :])
                    ins.then_inc(s_afull, 1)
                pe.wait_ge(s_afree, base + DC)
                for i in range(NI):
                    for c in range(DC):
                        ins = pe.matmul(bankL[:, i * E:(i + 1) * E], h2T[:, c, i * P:(i + 1) * P], gwT[:, c, :],
                                        start=(c == 0), stop=(c == DC - 1))
                ins.then_inc(s_log, 1)
                pe.wait_ge(s_oh, bb + 1)
                oh = onehot[:, :, :].rearrange("p i e -> p (i e)")
                pe.matmul(bankL[:, 64:64 + NI * E], triu[:, :], oh, start=True, stop=True)
                pe.matmul(bankL[:, 128:128 + NI * E], ones[:, :], oh, start=True, stop=True).then_inc(s_cnt, 1)

            with pe.Fori(0, HB_ - 1) as i:
                for k in (0, 1):
                    batch(2 * i + k, k, False)
            batch(B - 2, 0, False)
            batch(B - 1, 1, True)
            pe.wait_ge(s_slot, B)

            pe.wait_ge(s_tiles, 1)

            def by_tiles(n, emit):
                with pe.If(n < NW):
                    emit(NW - 1)
                with pe.Else():
                    with pe.If(n < NS):
                        emit(NW)
                    with pe.Else():
                        emit(NS)

            def fill(n, b, j=None):
                pe.wait_ge(s_hx, n + 1)
                if j is None:
                    if n > 1:
                        pe.wait_ge(s_xl, n - 1)
                else:
                    pe.wait_ge(s_hf, HP * (j + 1) + b + 1)
                for c in range(DC):
                    ins = pe.transpose(bankH[b][:, c * P:(c + 1) * P], hx[b][:, c * P:(c + 1) * P], ident[:, :])
                ins.then_inc(s_xf, 1)

            def up(e, j, k, n, fills):
                pe.wait_ge(s_w1l, j + 1)
                pe.wait_ge(s_xl, fills)
                pe.wait_ge(s_hf, HP * (j + 1))

                def product(dst, f, a, z):
                    for c in range(DC):
                        for m, (wt, xt) in enumerate(((w1h, xh), (w1h, xl), (w1l, xh))):
                            ins = pe.matmul(dst, wt[k][:, c, f * P:(f + 1) * P],
                                            xt[:, ds(e % 2, 1), c, a:z].rearrange("p k n -> p (k n)"),
                                            start=(c == 0 and m == 0), stop=(c == DC - 1 and m == 2))
                    return ins

                def emit(tiles):
                    wide = min(tiles, NW) * P
                    for f in range(QF):
                        product(bankH[f][:, 0:wide], f, 0, wide).then_inc(s_up, 1)
                    if tiles > NW:
                        for f in range(QF):
                            ins = product(bankH4[:, f * P:(f + 1) * P], f, WIDE, CAP)
                        ins.then_inc(s_up, 1)
                    else:
                        pe.matmul(bankH4[:, 0:P], w1h[k][:, 0, 0:P],
                                  xh[:, ds(e % 2, 1), 0, WIDE:CAP].rearrange("p k n -> p (k n)"),
                                  start=True, stop=True).then_inc(s_up, 1)

                by_tiles(n, emit)

            def down(j, k, n, first=False, between=None):
                pe.wait_ge(s_w2l, j + 1)
                pe.wait_ge(s_hl, HP * (j + 2))

                def emit(tiles):
                    for f in range(QF):
                        if f == QF - 1 and between is not None:
                            between()
                        for s in range(tiles):
                            for m, (ht, wt) in enumerate(((hh, w2h), (hh, w2l), (hl, w2h))):
                                ins = pe.matmul(bankY[:, s, :], ht[k][:, f, s * P:(s + 1) * P], wt[k][:, f, :],
                                                start=(first and f == 0 and m == 0), stop=True,
                                                skip_group_check=True)
                    ins.then_inc(s_dn, 1)

                by_tiles(n, emit)

            def expert(e, last):
                n = pe.value_load(tiles_ctl[0:1, ds(e, 1)], min_val=1, max_val=NS)
                base = (e + 1) * len(FILLS)
                up(e, e * NU + 1, 1, n, base)
                pe.wait_ge(s_yr, e * NS + 1)
                down(e * NU, 0, n, first=True)

                def pair(j, b):
                    up(e, j, 0, n, b)
                    if not last:
                        fill(b, 0, j)
                    down(j - 1, 1, n, between=None if last else lambda: fill(b + 1, 1, j))
                    up(e, j + 1, 1, n, base if last else b + 2)
                    down(j, 0, n)

                with pe.Fori(0, NU // 2 - 1) as p:
                    pair(e * NU + 2 * p + 2, base if last else base + 2 * p)
                if not last:
                    n_next = pe.value_load(tiles_ctl[0:1, ds(e + 1, 1)], min_val=1, max_val=NS)
                    up(e + 1, (e + 1) * NU, 0, n_next, base + len(FILLS))
                down(e * NU + NU - 1, 1, n)

            for m in range(len(FILLS)):
                fill(m, m % 2)
            n_first = pe.value_load(tiles_ctl[0:1, 0:1], min_val=1, max_val=NS)
            up(0, 0, 0, n_first, len(FILLS))
            with pe.Fori(0, E - 1) as e:
                expert(e, False)
            expert(E - 1, True)


_INS = ['x', 'ctx_1024', 'mask_BxS2_ik0', 'L0_xattn_Ws', 'L0_xattn_W', 'L0_xattn_w', 'L0_xattn_b', 'L0_xattn_Wcw',
        'L0_xattn_bcw', 'L0_xattn_Wcb', 'L0_xattn_bcb', 'L0_ffn_gate_w', 'L0_ffn_gate_b', 'L0_ffn_w1', 'L0_ffn_b1',
        'L0_ffn_w2', 'L0_ffn_b2']


def kernel(**inputs):
    import numpy as _np
    import concourse.bacc as _bacc
    from concourse import mybir as _mybir
    from concourse.bass_utils import run_bass_kernel_spmd as _run

    nc = _bacc.Bacc("TRN2", target_bir_lowering=False, num_devices=1)
    arrays, args = {}, []
    for name in _INS:
        a = _np.ascontiguousarray(inputs[name])
        arrays[f"in_{name}_dram"] = a
        args.append(nc.dram_tensor(f"in_{name}_dram", a.shape, _mybir.dt.from_np(a.dtype), kind="ExternalInput").ap())
    shape = inputs['x'].shape
    out = nc.dram_tensor("out_0_dram", shape, _mybir.dt.float32, kind="ExternalOutput").ap()
    xattn_moe_kernel(nc, *args, out)
    r = _run(nc, [arrays], core_ids=[0])
    return r.results[0]["out_0_dram"]
```

```python
import concourse.bass as bass
from concourse import mybir
from contextlib import ExitStack


def xattn_moe_kernel(nc, x, ctx, mask, Ws, W, w, b, Wcw, bcw, Wcb, bcb, gate_w, gate_b, w1, b1, w2, b2, out):
    fp32 = mybir.dt.float32
    i32 = mybir.dt.int32
    u32 = mybir.dt.uint32
    f32r = mybir.dt.float32r
    ALU = mybir.AluOpType
    ACT = mybir.ActivationFunctionType
    X = mybir.AxisListType.X
    ds = bass.ds

    P = 128
    B, S, D = x.shape
    T = ctx.shape[1]
    E, _, FF = w1.shape
    DC = D // P
    NI = S // P
    NF = FF // P
    TOK = B * S
    CAP = -(-5 * TOK // (4 * E))
    NS = CAP // P
    assert NS * P == CAP and NF % 8 == 0 and B % 2 == 0
    G = 4
    NG = -(-T // G)
    TP = NG * G
    HB_ = B // 2
    EPS = 1e-5
    NEG = 1e30
    BIG = 1.0e6
    MAGIC = 1597463007.0
    PAY = D + 4
    QF = 2
    NU = NF // QF
    NW = 4
    assert NU % 2 == 0 and NS == NW + 1 and NU >= 4

    buf = nc.dram_tensor("dispatched", (E * CAP, PAY), fp32, kind="Internal").ap()
    out_rows = out.rearrange("b s d -> (b s) d")

    st = ExitStack()
    with st:
        def sb(name, shape, dt=fp32):
            return st.enter_context(nc.sbuf_tensor(name, shape, dt))

        def sem(name):
            return st.enter_context(nc.semaphore(name))

        def phase():
            return st.enter_context(ExitStack())

        def part(stack, name, shape, dt=fp32):
            return stack.enter_context(nc.sbuf_tensor(name, shape, dt))[(slice(None),) * len(shape)]

        b1T = sb("b1T", [P, E * NF])
        tiles_ctl = sb("tiles_ctl", [1, E], i32)
        slot_idx = [sb(f"slot_idx{k}", [P, NI], u32) for k in (0, 1)]
        ident = sb("ident", [P, P])
        triu = sb("triu", [P, P])
        ones = sb("ones", [P, P])
        onesel = sb("onesel", [P, G, G])
        wsel = sb("wsel", [P, G, G])
        w_col = sb("w_col", [P, DC])
        b_col = sb("b_col", [P, DC])
        wc_col = sb("wc_col", [P, 2, DC])
        bc_col = sb("bc_col", [P, 2])
        gwT_high = sb("gwT_high", [P, DC, E], f32r)
        gwT_low = sb("gwT_low", [P, DC, E], f32r)
        gb_row = sb("gb_row", [P, E])
        mask_i = sb("mask_i", [T, B], i32)
        maskf = sb("maskf", [T, B])
        active = sb("active", [T, B])
        kpos = sb("kpos", [T, 4, B])
        t_index = sb("t_index", [P, 1])
        col_index = sb("col_index", [P, P])
        group_edge = sb("group_edge", [1, B, NG])
        past_edge = sb("past_edge", [1, B, NG])
        counts = sb("counts", [1, 4, B])
        ctl = sb("ctl", [1, 2, B], i32)
        erev = sb("erev", [P, E])
        ebase = sb("ebase", [P, E])
        tokid = sb("tokid", [P, NI])

        ln_st = sb("ln_st", [P, B, NI, 6])
        ln_mv = sb("ln_mv", [P, B, NI, 2])
        mean_x = sb("mean_x", [P, B, NI])
        var_x = sb("var_x", [P, B, NI])
        rstd_x = sb("rstd_x", [P, B, NI], i32)
        std_x = sb("std_x", [P, B, NI])
        shift_x = sb("shift_x", [P, B, NI])
        rsq_v = sb("rsq_v", [P, B, NI])
        rsq_t = sb("rsq_t", [P, 2, B, NI])
        rstd_2 = sb("rstd_2", [P, 1, NI], i32)
        affine = sb("affine", [P, 6, NI])
        mx = sb("mx", [P, NI])
        nd = sb("nd", [P, 3, NI])
        rden = sb("rden", [P, NI])
        ws_in = sb("ws_in", [P, 2, NI])
        ws = sb("ws", [P, 2, NI])
        lg = sb("lg", [P, NI, E])
        lgd = sb("lgd", [P, NI, E])
        lraw = [sb(f"lraw{k}", [P, NI, E]) for k in (0, 1)]
        counts_in = sb("counts_in", [P, 2, NI, E])
        lge = sb("lge", [P, NI, E])
        eq = sb("eq", [P, NI, E])
        onehot = sb("onehot", [P, NI, E])
        top = sb("top", [P, 2, NI])
        psum_e = sb("psum_e", [P, NI])
        run = sb("run", [P, NI + 1, E])
        cume = sb("cume", [P, 2, NI, E])
        pos = sb("pos", [P, 5, NI])
        out_idx = sb("out_idx", [P, NS], u32)
        load_n = sb("load_n", [1, 3, E])
        tile_edge = sb("tile_edge", [1, E, NS - 1])
        past_tile = sb("past_tile", [1, E, NS - 1])

        attention = phase()

        prelude = phase()
        Ws_sb = part(prelude, "Ws_sb", [P, DC, D])
        ctx_sb = part(prelude, "ctx_sb", [T, B, D])
        W_sb = part(prelude, "W_sb", [P, DC, D])
        perm = part(prelude, "perm", [T, B, T])
        wc_wide = part(prelude, "wc_wide", [P, 2, DC, P])
        ctxT = part(prelude, "ctxT", [P, DC, B, T])
        maskw = part(prelude, "maskw", [T, B, P])
        b1rows = part(prelude, "b1rows", [E * NF, P])
        gw_rows = part(prelude, "gw_rows", [E, D])
        blank = part(prelude, "blank", [P, PAY])
        prelude.close()

        h_ring = part(attention, "h_ring", [P, G, DC, S])
        partial = part(attention, "partial", [P, 2, S])
        rho_rows = part(attention, "rho_rows", [G, S])
        z = part(attention, "z", [P, NI, T])
        pw = part(attention, "pw", [P, 2, NI, T])
        pay = [part(attention, f"pay{k}", [P, NI, PAY]) for k in (0, 1)]
        logit_rows = part(attention, "logit_rows", [E, S])

        W_high = part(attention, "W_high", [P, DC, D], f32r)
        W_low = part(attention, "W_low", [P, DC, D], f32r)
        xn = part(attention, "xn", [P, NI, D])
        xnT_high = part(attention, "xnT_high", [P, DC, S], f32r)
        xnT_low = part(attention, "xnT_low", [P, DC, S], f32r)
        featT = [part(attention, f"featT{k}", [P, DC, S]) for k in (0, 1)]
        txtT = part(attention, "txtT", [P, DC, B, TP])
        bias_row = part(attention, "bias_row", [P, B, T])
        cw_row = part(attention, "cw_row", [P, B, T])
        cb_row = part(attention, "cb_row", [P, B, T])
        x_all = part(attention, "x_all", [P, B, NI, D])
        attention.close()

        experts = phase()
        w1s = [part(experts, f"w1s{k}", [P, DC, QF * P]) for k in (0, 1)]
        w2s = [part(experts, f"w2s{k}", [P, QF, D]) for k in (0, 1)]
        xin = part(experts, "xin", [P, 2, NS, PAY])
        hx = [part(experts, f"hx{k}", [P, D]) for k in (0, 1)]
        y_out = part(experts, "y_out", [P, NS, D])
        b2wide = part(experts, "b2wide", [P, 2, D])
        relu_out = part(experts, "relu_out", [P, QF, CAP])
        xh = part(experts, "xh", [P, 2, DC, CAP], f32r)
        xl = part(experts, "xl", [P, 2, DC, CAP], f32r)
        w1h = [part(experts, f"w1h{k}", [P, DC, QF * P], f32r) for k in (0, 1)]
        w1l = [part(experts, f"w1l{k}", [P, DC, QF * P], f32r) for k in (0, 1)]
        w2h = [part(experts, f"w2h{k}", [P, QF, D], f32r) for k in (0, 1)]
        w2l = [part(experts, f"w2l{k}", [P, QF, D], f32r) for k in (0, 1)]
        hh = [part(experts, f"hh{k}", [P, QF, CAP], f32r) for k in (0, 1)]
        hl = [part(experts, f"hl{k}", [P, QF, CAP], f32r) for k in (0, 1)]

        PS = st.enter_context(nc.psum_tensor("PS", [P, 8, 512], fp32))
        bankA = [PS[:, q, :] for q in (0, 1, 6, 7)]
        bankP = [PS[:, 2, :], PS[:, 3, :]]
        bankR = PS[0:G, 2:4, :]
        bankT = PS[:, 4, :]
        bankL = PS[:, 5, :]
        bankY = PS[:, 0:NS, :]
        bankH = [PS[:, 5, :], PS[:, 6, :]]
        bankH4 = PS[:, 7, :]

        s_const = sem("const_built")
        s_mask = sem("mask_loaded")
        s_ctx = sem("keys_loaded")
        s_Ws = sem("key_projection_loaded")
        s_ldw = sem("small_weights_loaded")
        s_ldW = sem("W_loaded")
        s_x = [sem(f"x_loaded_{n}") for n in range(B)]
        s_blank = sem("slots_blanked")
        s_pre = sem("prelude_dve_step")
        s_preA = sem("prelude_bank_filled")
        s_preF = sem("prelude_bank_read")
        s_lateF = sem("gates_and_b1_read")
        s_preA2 = sem("attended_keys_counted")
        s_perm = sem("permutations_built")
        s_gw = sem("gate_weights_transposed")
        s_gwr = sem("gate_weights_in_sbuf")
        s_wide = sem("wide_columns_built")
        s_ctl = sem("group_counts_ready")
        s_xn = sem("xn_ready")
        s_xnhigh = sem("xnT_high_parts_ready")
        s_Wsplit = sem("W_split")
        s_clear = sem("psum_cleared")
        s_afull = sem("bankA_filled")
        s_afree = sem("bankA_read")
        s_h = sem("tanh_ready")
        s_sum = sem("partial_ready")
        s_gch = sem("partial_chain")
        s_hfree = sem("rho_key_done")
        s_rfree = sem("bankR_read")
        s_row = sem("rho_group_transposed")
        s_ep = sem("epilogue_chain")
        s_zs = sem("scores_shifted")
        s_exp = sem("exp_done")
        s_wsin = sem("gates_in_ready")
        s_ws = sem("gates_ready")
        s_x2 = sem("x2_ready")
        s_lprod = sem("logit_rows_in_psum")
        s_lrows = sem("logit_rows_ready")
        s_lraw = sem("raw_logits_ready")
        s_lread = sem("bankL_read")
        s_lgd = sem("logits_shifted")
        s_lge = sem("logits_exp_done")
        s_gsum = sem("exp_sums_ready")
        s_affine = sem("scale_and_offset_ready")
        s_lnx = sem("x_statistics_ready")
        s_run = sem("slot_chain")
        s_ready = sem("slots_computed")
        s_oh = sem("onehot_ready")
        s_cnt = sem("expert_counts_ready")
        s_slot = sem("slots_ready")
        s_store = [sem(f"x2_stored_{k}") for k in (0, 1)]
        s_scat = sem("rows_dispatched")
        s_payfree = sem("payload_dispatched")
        s_yfree = sem("expert_buffer_written_out")
        s_w1 = [sem(f"w1_unit_loaded_{k}") for k in (0, 1)]
        s_w2 = [sem(f"w2_unit_loaded_{k}") for k in (0, 1)]
        s_w1h = sem("w1_high_parts_ready")
        s_w2h = sem("w2_high_parts_ready")
        s_w1l = sem("w1_split")
        s_w2l = sem("w2_split")
        s_b2 = sem("b2_loaded")
        s_xin = sem("expert_rows_loaded")
        s_fin = sem("tile_count_chain")
        s_tiles = sem("slot_tiles_counted")
        s_hx = sem("slot_tile_normalised")
        s_xf = sem("slot_tile_transposed")
        s_xh = sem("x_high_parts_ready")
        s_xl = sem("x_split")
        s_up = sem("hidden_in_psum")
        s_hf = sem("hidden_read")
        s_hh = sem("hidden_high_parts_ready")
        s_hl = sem("hidden_split")
        s_dn = sem("unit_added_to_output")
        s_u = sem("residual_rows_ready")
        s_yr = sem("expert_output_read")
        s_yo = sem("expert_rows_written")

        rawL = bankL[:, 0:NI * E].rearrange("p (i e) -> p i e", i=NI)
        cntL = bankL[:, NI * E:3 * NI * E].rearrange("p (q i e) -> p q i e", q=2, i=NI)

        def z_half(rows, hf):
            return rows[:, hf * HB_:(hf + 1) * HB_, :].rearrange("p b t -> p (b t)")

        WIDE = NW * P
        HP = QF + 1
        FILLS = [s for p in range(NU // 2 - 1) for s in (p, p + 2)]
        assert sorted(set(FILLS)) == list(range(NS))
        PRE_FILLS = B + 2 + 2 * DC
        EPI_STEPS = 31
        RUN_STEPS = 14

        def wait_apart(engine, semaphore, value):
            value = value if isinstance(value, int) else engine.to_reg(value)
            engine.wait_ge(s_const, 1)
            engine.wait_ge(semaphore, value)

        block = st.enter_context(nc.Block())

        @block.sync
        def _(sp):
            def load_x(n):
                sp.dma_start(x_all[:, n, :, :], x[n].rearrange("(i p) d -> p i d", p=P)).then_inc(s_x[n], 16)

            sp.dma_start(mask_i[:, :], mask.rearrange("b t -> t b"), allow_slow_non_contiguous=True)\
              .then_inc(s_mask, 16)
            load_x(0)
            sp.dma_start(ctx_sb, ctx.rearrange("b t d -> t b d")).then_inc(s_ctx, 16)
            sp.dma_start(W_sb[:, :, :], W.rearrange("(c p) e -> p c e", p=P)).then_inc(s_ldW, 16)
            sp.dma_start(Ws_sb, Ws.rearrange("(c p) e -> p c e", p=P)).then_inc(s_Ws, 16)
            for n in range(1, B):
                load_x(n)

            def load_w1(e, i, k):
                sp.dma_start(w1s[k][:, :, :], w1[ds(e, 1), :, ds(i * QF * P, QF * P)]
                             .rearrange("e (c p) f -> p (e c) f", p=P)).then_inc(s_w1[k], 16)

            def load_w2(e, i, k):
                sp.dma_start(w2s[k][:, :, :], w2[ds(e, 1), ds(i * QF * P, QF * P), :]
                             .rearrange("e (g p) d -> p (e g) d", p=P)).then_inc(s_w2[k], 16)

            def batch(bb, k):
                sp.wait_ge(s_x2, bb + 1)
                sp.dma_start(out[bb].rearrange("(i p) d -> p i d", p=P), pay[k][:, :, 0:D]).then_inc(s_store[k], 16)

            with sp.Fori(0, HB_) as i:
                for k in (0, 1):
                    batch(2 * i + k, k)
            sp.wait_ge(s_zs, B)
            for k in (0, 1):
                load_w1(0, k, k)
                load_w2(0, k, k)

            def load_rows(e):
                sp.dma_start(xin[:, ds(e % 2, 1), :, :].rearrange("p k s d -> p (k s) d"),
                             buf[ds(e * CAP, CAP), :].rearrange("(s p) d -> p s d", p=P)).then_inc(s_xin, 16)
                sp.dma_start(b2wide[:, ds(e % 2, 1), :].rearrange("p k d -> p (k d)"),
                             b2[ds(e, 1), :].broadcast_to([P, D])).then_inc(s_b2, 16)

            sp.wait_ge(s_slot, B + 1)
            sp.wait_ge(s_scat, B * NI * 16)
            sp.wait_ge(s_tiles, 1)
            for k in (0, 1):
                sp.wait_ge(s_store[k], HB_ * 16 + 16)
            load_rows(0)

            def expert(e, last):
                def ahead(j, i, k, e_to, i_to, rows=False):
                    sp.wait_ge(s_w1l, j + 1)
                    load_w1(e_to, i_to, k)
                    if rows:
                        sp.wait_ge(s_yr, e * NS + 1)
                        load_rows(e + 1)
                    sp.wait_ge(s_w2l, j + 1)
                    load_w2(e_to, i_to, k)

                ahead(e * NU, 0, 0, e, 2)
                ahead(e * NU + 1, 1, 1, e, 3, rows=not last)
                with sp.Fori(0, NU // 2 - 2) as p:
                    for k in (0, 1):
                        ahead(e * NU + 2 * p + 2 + k, 2 * p + 2 + k, k, e, 2 * p + 4 + k)
                if not last:
                    for k in (0, 1):
                        ahead(e * NU + NU - 2 + k, NU - 2 + k, k, e + 1, k)

            with sp.Fori(0, E - 1) as e:
                expert(e, False)
            expert(E - 1, True)
            for k in (0, 1):
                sp.wait_ge(s_store[k], HB_ * 16 + 16)
            sp.wait_ge(s_yo, E * NS * 16)
            sp.wait_ge(s_blank, 16)

        @block.gpsimd
        def _(pool):
            pool.memset(ones[:, :], 1.0).then_inc(s_const, 1)
            pool.memset(ident[:, :], 0.0).then_inc(s_const, 1)
            pool.memset(blank[:, :], 0.0).then_inc(s_const, 1)
            pool.memset(onesel[:, :, :], 0.0).then_inc(s_const, 1)
            pool.memset(txtT[:, :, :, T:TP], 0.0).then_inc(s_const, 1)
            pool.memset(run[:, :, :], 0.0).then_inc(s_const, 1)
            pool.iota(col_index[:, :], pattern=[[1, P]], base=0, channel_multiplier=0,
                      allow_small_or_imprecise_dtypes=True).then_inc(s_const, 1)
            pool.iota(t_index[:, :], pattern=[[0, 1]], base=0, channel_multiplier=1,
                      allow_small_or_imprecise_dtypes=True).then_inc(s_const, 1)
            pool.iota(group_edge[:, :, :], pattern=[[0, B], [G, NG]], base=0, channel_multiplier=0,
                      allow_small_or_imprecise_dtypes=True).then_inc(s_const, 1)
            pool.iota(erev[:, :], pattern=[[-1, E]], base=E, channel_multiplier=0,
                      allow_small_or_imprecise_dtypes=True).then_inc(s_const, 1)
            pool.iota(ebase[:, :], pattern=[[CAP, E]], base=0, channel_multiplier=0,
                      allow_small_or_imprecise_dtypes=True).then_inc(s_const, 1)
            pool.iota(tile_edge[:, :, :], pattern=[[0, E], [P, NS - 1]], base=P, channel_multiplier=0,
                      allow_small_or_imprecise_dtypes=True).then_inc(s_const, 1)
            pool.iota(tokid[:, :], pattern=[[P, NI]], base=0, channel_multiplier=1,
                      allow_small_or_imprecise_dtypes=True).then_inc(s_const, 1)
            pool.wait_ge(s_const, 13)
            pool.affine_select(out=ident[:, :], in_=ident[:, :], compare_op=ALU.not_equal, fill=1.0,
                               base=0, pattern=[[-1, P]], channel_multiplier=1).then_inc(s_const, 1)
            pool.affine_select(out=triu[:, :], in_=ones[:, :], compare_op=ALU.is_ge, fill=0.0,
                               base=0, pattern=[[1, P]], channel_multiplier=-1).then_inc(s_const, 1)
            pool.affine_select(out=onesel[:, :, :], in_=onesel[:, :, :], compare_op=ALU.not_equal, fill=1.0,
                               base=0, pattern=[[1, G], [-1, G]], channel_multiplier=0).then_inc(s_const, 1)
            pool.memset(blank[:, PAY - 1:PAY], BIG).then_inc(s_const, 1)
            for k in (0, 1):
                pool.sem_inc(s_store[k], 16)
            pool.sem_inc(s_yfree, 1)
            pool.wait_ge(s_const, 17)
            pool.wait_ge(s_ldw, 9 * 16)
            pool.wait_ge(s_x[B - 1], 16)
            pool.dma_start(buf.rearrange("(s p) d -> p s d", p=P),
                           blank[:, None, :].broadcast_to([P, E * NS, PAY])).then_inc(s_blank, 16)
            pool.wait_ge(s_blank, 16)
            pool.sem_inc(s_payfree, 2)

            def batch(bb, k):
                wait_apart(pool, s_lread, bb + 3)
                step = 0

                def link(ins):
                    nonlocal step
                    step += 1
                    ins.then_inc(s_run, 1)
                    wait_apart(pool, s_run, bb * RUN_STEPS + step)

                cnt, tot = counts_in[:, 0, :, :], counts_in[:, 1, :, :]
                link(pool.tensor_copy(run[:, 0, :], run[:, NI, :]))
                for i in range(NI):
                    link(pool.tensor_tensor(run[:, i + 1, :], run[:, i, :], tot[:, i, :], ALU.add))
                link(pool.tensor_tensor(cume[:, 0, :, :], cnt, run[:, 0:NI, :], ALU.add))
                pool.tensor_tensor(cume[:, 1, :, :], onehot[:, :, :],
                                   ebase[:, None, :].broadcast_to([P, NI, E]), ALU.mult)
                link(pool.tensor_tensor(cume[:, 0, :, :], cume[:, 0, :, :], onehot[:, :, :], ALU.mult))
                half = E // 2
                while half:
                    link(pool.tensor_tensor(cume[:, :, :, 0:half], cume[:, :, :, 0:half],
                                            cume[:, :, :, half:2 * half], ALU.add))
                    half //= 2
                before, base = cume[:, 0, :, 0], cume[:, 1, :, 0]
                pool.tensor_scalar(pos[:, 2, :], before, float(CAP), BIG, ALU.is_gt, ALU.mult)
                link(pool.tensor_tensor(pos[:, 0, :], before, base, ALU.add))
                link(pool.tensor_scalar(pos[:, 1, :], pos[:, 0, :], -1.0, None, ALU.add))
                link(pool.tensor_tensor(pos[:, 4, :], pos[:, 1, :], pos[:, 2, :], ALU.add))
                link(pool.tensor_copy(slot_idx[k][:, :], pos[:, 4, :]))
                assert step == RUN_STEPS, step
                pool.sem_inc(s_ready, 1)
                wait_apart(pool, s_x2, bb + 1)
                wait_apart(pool, s_slot, bb + 2)
                for i in range(NI):
                    pool.indirect_dma_start(buf, bass.IndirectOffsetOnAxis(ap=slot_idx[k][:, i:i + 1], axis=0),
                                            pay[k][:, i, :], None, bounds_check=E * CAP - 1,
                                            oob_is_err=False).then_inc(s_scat, 16)
                pool.wait_ge(s_scat, (bb + 1) * NI * 16)
                pool.sem_inc(s_payfree, 1)

            with pool.Fori(0, HB_) as i:
                for k in (0, 1):
                    batch(2 * i + k, k)

            for k in (0, 1):
                pool.wait_ge(s_store[k], HB_ * 16 + 16)
            with pool.Fori(0, E) as e:
                for s in range(NS):
                    wait_apart(pool, s_yr, e * NS + s + 2)
                    pool.indirect_dma_start(out_rows, bass.IndirectOffsetOnAxis(ap=out_idx[:, s:s + 1], axis=0),
                                            y_out[:, s, :], None, bounds_check=TOK - 1,
                                            oob_is_err=False).then_inc(s_yo, 16)
                pool.wait_ge(s_yo, (e + 1) * NS * 16)
                pool.sem_inc(s_yfree, 1)

        @block.scalar
        def _(act):
            act.dma_start(gw_rows[:, :], gate_w).then_inc(s_ldw, 16)
            act.dma_start(b1rows[:, :], b1.rearrange("e (f p) -> (e f) p", p=P)).then_inc(s_ldw, 16)
            act.dma_start(w_col[:, :], w.rearrange("(c p) o -> p (c o)", p=P),
                          allow_slow_non_contiguous=True).then_inc(s_ldw, 16)
            act.dma_start(b_col[:, :], b.rearrange("o (c p) -> p (o c)", p=P),
                          allow_slow_non_contiguous=True).then_inc(s_ldw, 16)
            act.dma_start(wc_col[:, 0, :], Wcw.rearrange("o (c p) -> p (o c)", p=P),
                          allow_slow_non_contiguous=True).then_inc(s_ldw, 16)
            act.dma_start(wc_col[:, 1, :], Wcb.rearrange("o (c p) -> p (o c)", p=P),
                          allow_slow_non_contiguous=True).then_inc(s_ldw, 16)
            act.dma_start(bc_col[:, 0:1], bcw.rearrange("(a o) -> a o", a=1).broadcast_to([P, 1])).then_inc(s_ldw, 16)
            act.dma_start(bc_col[:, 1:2], bcb.rearrange("(a o) -> a o", a=1).broadcast_to([P, 1])).then_inc(s_ldw, 16)
            act.dma_start(gb_row[:, :], gate_b.rearrange("(a o) -> a o", a=1).broadcast_to([P, E])).then_inc(s_ldw, 16)

            def x_highs(n):
                for c in range(DC):
                    wait_apart(act, s_afull, n * 2 * DC + c + 1)
                    act.activation(xnT_high[:, c, :], bankA[c], ACT.Copy).then_inc(s_xnhigh, 1)

            def column(tensor, n, i):
                return tensor[:, ds(n, 1), i:i + 1].rearrange("p b i -> p (b i)")

            def normalise(n):
                for i in range(NI):
                    ins = act.activation(xn[:, i, :], x_all[:, ds(n, 1), i, :].rearrange("p b d -> p (b d)"),
                                         ACT.Identity, bias=column(shift_x, n, i),
                                         scale=column(rstd_x.bitcast(fp32), n, i))
                ins.then_inc(s_xn, 1)

            f = 0

            def filled():
                nonlocal f
                f += 1
                act.wait_ge(s_preA, f)
                return bankP[(f - 1) % 2]

            for n in range(B):
                bk = filled()
                act.activation(ctxT[:, :, n, :], bk[:, 0:DC * T].rearrange("p (c t) -> p c t", c=DC),
                               ACT.Copy).then_inc(s_preF, 1)
            for hf in (0, 1):
                bk = filled()
                act.activation(z_half(bias_row, hf), bk[:, 0:HB_ * T], ACT.Copy).then_inc(s_preF, 1)
            act.wait_ge(s_ldW, 16)
            act.activation(W_high[:, :, :], W_sb[:, :, :], ACT.Copy).then_inc(s_Wsplit, 1)
            act.wait_ge(s_ldw, 9 * 16)
            for c in range(DC):
                for hf in (0, 1):
                    bk = filled()
                    act.activation(txtT[:, c, hf * HB_:(hf + 1) * HB_, 0:T],
                                   bk[:, 0:HB_ * T].rearrange("p (b t) -> p b t", b=HB_),
                                   ACT.Identity, bias=b_col[:, c:c + 1]).then_inc(s_preF, 1)
            assert f == PRE_FILLS
            act.wait_ge(s_preF, PRE_FILLS)
            x_highs(0)
            act.wait_ge(s_Wsplit, 2)
            x_highs(1)
            act.wait_ge(s_lnx, 4)
            normalise(2)
            act.wait_ge(s_ctl, 1)

            def gate_exp(bb):
                act.wait_ge(s_lgd, bb + 1)
                act.activation(lge[:, :, :], lgd[:, :, :], ACT.Exp).then_inc(s_lge, 1)

            def batch(bb, ib, k, last):
                n = act.value_load(ctl[0:1, 0, ds(bb, 1)], min_val=1, max_val=NG)
                k0 = act.value_load(ctl[0:1, 1, ds(bb, 1)], min_val=0, max_val=B * NG)
                wait_apart(act, s_afree, 2 * DC * (bb + 1))
                with act.Fori(0, n) as g:
                    for t in range(G):
                        wait_apart(act, s_hfree, (k0 + g) * G + t + 1)
                        for c in range(DC):
                            ins = act.activation(h_ring[:, t, c, :], featT[k][:, c, :], ACT.Tanh,
                                                 bias=txtT[:, c, ds(bb, 1), ds(g * G + t, 1)].rearrange("p b t -> p (b t)"))
                        ins.then_inc(s_h, 1)
                if not last:
                    x_highs(bb + 2)
                act.wait_ge(s_zs, bb + 1)
                act.activation(z[:, :, :], z[:, :, :], ACT.Exp).then_inc(s_exp, 1)
                gate_exp(bb)
                if not last:
                    normalise((bb + 3) % B)
                act.wait_ge(s_wsin, bb + 1)
                for m in (0, 1):
                    act.activation(ws[:, m, :], ws_in[:, m, :], ACT.Tanh, bias=bc_col[:, m:m + 1]).then_inc(s_ws, 1)
                act.wait_ge(s_payfree, bb + 1)
                act.wait_ge(s_store[k], ib * 16 + 16)
                wait_apart(act, s_affine, bb + 1)
                for i in range(NI):
                    ins = act.activation(pay[k][:, i, 0:D], x_all[:, ds(bb, 1), i, :].rearrange("p b d -> p (b d)"),
                                         ACT.Identity, bias=affine[:, 1, i:i + 1], scale=affine[:, 0, i:i + 1])
                ins.then_inc(s_x2, 1)

            with act.Fori(0, HB_ - 1) as i:
                for k in (0, 1):
                    batch(2 * i + k, i, k, False)
            for k in (0, 1):
                batch(B - 2 + k, HB_ - 1, k, True)
            gate_exp(B)

            act.wait_ge(s_tiles, 1)

            def w1_high(j, k, n):
                act.wait_ge(s_w1[k], (n + 1) * 16)
                act.wait_ge(s_up, HP * j + HP)
                act.activation(w1h[k][:, :, :], w1s[k][:, :, :], ACT.Copy).then_inc(s_w1h, 1)

            def w2_high(j, k, n):
                act.wait_ge(s_w2[k], (n + 1) * 16)
                act.wait_ge(s_dn, j + 1)
                act.activation(w2h[k][:, :, :], w2s[k][:, :, :], ACT.Copy).then_inc(s_w2h, 1)

            def hidden(j):
                for m in range(HP):
                    act.wait_ge(s_hl, HP * j + m + 1)
                    wait_apart(act, s_up, HP * (j + 2) + m + 1)
                    for f in ([m] if m < QF else range(QF)):
                        if m < QF:
                            src, cols = bankH[f], slice(0, WIDE)
                        else:
                            src, cols = bankH4[:, f * P:(f + 1) * P], slice(WIDE, CAP)
                        ins = act.activation(relu_out[:, f, cols], src, ACT.Relu, bias=b1T[:, ds(j * QF + f, 1)])
                    ins.then_inc(s_hf, 1)

            def x_high(fill, e, s, bank):
                act.wait_ge(s_xf, fill + 1)
                act.activation(xh[:, ds(e % 2, 1), :, ds(s * P, P)].rearrange("p k c n -> p (k c) n"),
                               bankH[bank].rearrange("p (c n) -> p c n", c=DC), ACT.Copy).then_inc(s_xh, 1)

            w1_high(0, 0, 0)
            for s in range(NS):
                x_high(s, 0, s, s % 2)

            def first_turn(e):
                w1_high(e * NU + 1, 1, e * (NU // 2))
                hidden(e * NU)
                w2_high(e * NU, 0, e * (NU // 2))

            def expert(e, last):
                w1_high(e * NU + 2, 0, e * (NU // 2) + 1)
                hidden(e * NU + 1)
                w2_high(e * NU + 1, 1, e * (NU // 2))
                with act.Fori(0, NU // 2 - 2) as p:
                    j = e * NU + 2 * p + 2
                    n = e * (NU // 2) + p + 1
                    fill = NS + e * len(FILLS) + 2 * p
                    w1_high(j + 1, 1, n)
                    hidden(j)
                    if not last:
                        x_high(fill, e + 1, p, 0)
                    w2_high(j, 0, n)
                    if not last:
                        x_high(fill + 1, e + 1, p + 2, 1)
                    w1_high(j + 2, 0, n + 1)
                    hidden(j + 1)
                    w2_high(j + 1, 1, n)
                j = e * NU + NU - 2
                n = (e + 1) * (NU // 2) - 1
                fill = NS + (e + 1) * len(FILLS) - 2
                w1_high(j + 1, 1, n)
                hidden(j)
                if not last:
                    x_high(fill, e + 1, NU // 2 - 2, 0)
                w2_high(j, 0, n)
                if not last:
                    x_high(fill + 1, e + 1, NU // 2, 1)
                    w1_high(j + 2, 0, n + 1)
                hidden(j + 1)
                w2_high(j + 1, 1, n)
                if not last:
                    first_turn(e + 1)

            first_turn(0)
            with act.Fori(0, E - 1) as e:
                expert(e, False)
            expert(E - 1, True)

        @block.vector
        def _(dve):
            def wait(engine, semaphore, value):
                engine.wait_ge(semaphore, value)

            class Chain:

                def __init__(self, semaphore, base):
                    self.semaphore, self.base, self.n = semaphore, base, 0

                def link(self, ins, apart=False):
                    self.n += 1
                    ins.then_inc(self.semaphore, 1)
                    (wait_apart if apart else wait)(dve, self.semaphore, self.base + self.n)

            dve.sem_inc(s_rfree, 1)
            dve.sem_inc(s_hfree, G)
            dve.sem_inc(s_yr, 1)
            dve.sem_inc(s_ready, 1)
            dve.sem_inc(s_up, 2 * HP)
            dve.sem_inc(s_hf, HP)
            dve.sem_inc(s_hl, HP)
            dve.sem_inc(s_dn, 2)

            pre = Chain(s_pre, 0)
            dve.wait_ge(s_mask, 16)
            dve.wait_ge(s_const, 17)
            pre.link(dve.tensor_copy(maskf[:, :], mask_i[:, :]))
            dve.memset(PS[0:G, 3, :], 0.0)
            pre.link(dve.tensor_scalar(active[:, :], maskf[:, :], 0.0, None, ALU.is_gt))
            dve.wait_ge(s_preA2, 1)
            cnt_cum, cnt_all = bankT[0:T, 0:B], bankT[:, B:2 * B]
            pre.link(dve.tensor_copy(kpos[:, 3, :], cnt_cum))
            pre.link(dve.scalar_tensor_tensor(kpos[:, 0, :], bankT[0:T, B:2 * B], t_index[0:T, 0:1], kpos[:, 3, :],
                                              ALU.add, ALU.subtract))
            pre.link(dve.scalar_tensor_tensor(kpos[:, 1, :], kpos[:, 3, :], -1.0, kpos[:, 0, :],
                                              ALU.add, ALU.subtract))
            pre.link(dve.tensor_tensor(kpos[:, 2, :], kpos[:, 1, :], active[:, :], ALU.mult))
            pre.link(dve.tensor_tensor(kpos[:, 3, :], kpos[:, 2, :], kpos[:, 0, :], ALU.add))
            for n in range(B):
                dve.tensor_scalar(maskw[:, n, :], ones[0:T, :], maskf[:, n:n + 1], None, ALU.mult)
                ins = dve.tensor_scalar(perm[:, n, :], col_index[0:T, 0:T], kpos[:, 3, n:n + 1], None, ALU.is_equal)
            ins.then_inc(s_perm, 1)
            pre.link(dve.tensor_copy(counts[:, 0, :], bankT[0:1, B:2 * B]))
            pre.link(dve.tensor_tensor(past_edge[:, :, :], counts[:, 0, :][:, :, None].broadcast_to([1, B, NG]),
                                       group_edge[:, :, :], ALU.is_gt))
            pre.link(dve.tensor_reduce(counts[:, 1, :], past_edge[:, :, :], X, ALU.add))
            pre.link(dve.tensor_scalar(counts[:, 1, :], counts[:, 1, :], 1.0, None, ALU.max))
            pre.link(dve.tensor_tensor_scan(counts[:, 2, :], ones[0:1, 0:B], counts[:, 1, :], 0.0,
                                            ALU.mult, ALU.add))
            pre.link(dve.tensor_tensor(counts[:, 3, :], counts[:, 2, :], counts[:, 1, :], ALU.subtract))
            pre.link(dve.tensor_copy(ctl[:, 0, :], counts[:, 1, :]))
            pre.link(dve.tensor_copy(ctl[:, 1, :], counts[:, 3, :]))
            dve.nop().then_inc(s_ctl, 1)
            pre.link(dve.memset(bankT, 0.0))
            def rsqrt(chain, y_bits, var, n):
                v, t0, t1 = rsq_v[:, n, :], rsq_t[:, 0, n, :], rsq_t[:, 1, n, :]
                y = y_bits.bitcast(fp32)
                chain.link(dve.tensor_scalar(v, var, EPS, None, ALU.add))
                chain.link(dve.tensor_scalar(y_bits, v.bitcast(i32), -0.5, MAGIC, ALU.mult, ALU.add))
                for _ in range(3):
                    chain.link(dve.tensor_tensor(t0, y, y, ALU.mult))
                    chain.link(dve.scalar_tensor_tensor(t1, t0, -0.5, v, ALU.mult, ALU.mult))
                    chain.link(dve.scalar_tensor_tensor(y, t1, 1.5, y, ALU.add, ALU.mult))
                return y, v

            def moments(chain, batches):
                for n in batches:
                    dve.wait_ge(s_x[n], 16)
                    for i in range(NI):
                        ins = dve.bn_stats(ln_st[:, n, i, :], x_all[:, n, i, :])
                chain.link(ins)
                for n in batches:
                    for i in range(NI):
                        ins = dve.bn_aggr(ln_mv[:, n, i, :], ln_st[:, n, i, :])
                chain.link(ins)
                some = slice(batches[0], batches[-1] + 1)
                dve.tensor_copy(mean_x[:, some, :], ln_mv[:, some, :, 0])
                chain.link(dve.tensor_copy(var_x[:, some, :], ln_mv[:, some, :, 1]))
                y, v = rsqrt(chain, rstd_x[:, some, :], var_x[:, some, :], some)
                dve.scalar_tensor_tensor(shift_x[:, some, :], mean_x[:, some, :], -1.0, y, ALU.mult, ALU.mult)
                chain.link(dve.tensor_tensor(std_x[:, some, :], v, y, ALU.mult))
                dve.sem_inc(s_lnx, 1)

            def one(tensor, n):
                return tensor[:, ds(n, 1), :].rearrange("p b i -> p (b i)")

            def normalise(n):
                for i in range(NI):
                    ins = dve.tensor_scalar(xn[:, i, :], x_all[:, ds(n, 1), i, :].rearrange("p b d -> p (b d)"),
                                            one(mean_x, n)[:, i:i + 1], one(rstd_x.bitcast(fp32), n)[:, i:i + 1],
                                            ALU.subtract, ALU.mult)
                ins.then_inc(s_xn, 1)

            def x_lows(n):
                for c in range(DC):
                    wait_apart(dve, s_xnhigh, n * DC + c + 1)
                    dve.tensor_tensor(xnT_low[:, c, :], bankA[c], xnT_high[:, c, :].bitcast(fp32), ALU.subtract)\
                       .then_inc(s_afree, 1)

            def logit_evac(n):
                wait_apart(dve, s_lprod, n + 1)
                dve.tensor_copy(logit_rows[:, :], bankL[0:E, :]).then_inc(s_lrows, 1)

            def evac_f(n, k, c):
                wait_apart(dve, s_afull, n * 2 * DC + DC + c + 1)
                dve.tensor_copy(featT[k][:, c, :], bankA[c]).then_inc(s_afree, 1)

            def read_raw(n):
                dve.wait_ge(s_lraw, n + 1)
                dve.tensor_copy(lraw[n][:, :, :], rawL).then_inc(s_lread, 1)

            moments(pre, [0])
            normalise(0)
            moments(pre, [1])
            dve.wait_ge(s_Wsplit, 1)
            dve.tensor_tensor(W_low[:, :, :], W_sb[:, :, :], W_high[:, :, :].bitcast(fp32), ALU.subtract)\
               .then_inc(s_Wsplit, 1)
            dve.wait_ge(s_ldw, 9 * 16)
            for m in (0, 1):
                for c in range(DC):
                    dve.tensor_scalar(wc_wide[:, m, c, :], ones[:, :], wc_col[:, m, c:c + 1], None, ALU.mult)
            dve.tensor_scalar(wsel[:, :, :], onesel[:, :, :], w_col[:, 0:1], None, ALU.mult).then_inc(s_wide, 1)
            moments(pre, list(range(2, B - 2)))
            x_lows(0)
            dve.wait_ge(s_afull, DC)
            normalise(1)
            moments(pre, list(range(B - 2, B)))
            dve.wait_ge(s_preF, B + 2)
            pre.link(dve.tensor_scalar(bias_row[:, :, :], bias_row[:, :, :], -1.0, NEG, ALU.add, ALU.mult))
            for c in range(DC):
                evac_f(0, 0, c)
            dve.wait_ge(s_gw, 1)
            gate_psum = bankP[1][:, 0:DC * E].rearrange("p (c e) -> p c e", c=DC)
            pre.link(dve.tensor_copy(gwT_high[:, :, :], gate_psum))
            dve.tensor_tensor(gwT_low[:, :, :], gate_psum, gwT_high[:, :, :].bitcast(fp32), ALU.subtract)\
               .then_inc(s_gwr, 1)
            logit_evac(0)
            read_raw(0)
            x_lows(1)
            logit_evac(1)
            read_raw(1)
            late = 0
            for which in (cw_row, cb_row):
                for hf in (0, 1):
                    late += 1
                    dve.wait_ge(s_preA, PRE_FILLS + late)
                    dve.tensor_copy(z_half(which, hf), bankP[late % 2][:, 0:HB_ * T]).then_inc(s_lateF, 1)
            dve.wait_ge(s_preA, PRE_FILLS + late + 1)
            dve.tensor_copy(b1T[:, :], bankP[(late + 1) % 2][:, 0:E * NF]).then_inc(s_lateF, 1)

            def groups(bb, k, next_features):
                if next_features:
                    for c in range(DC - 1):
                        evac_f(bb + 1, 1 - k, c)
                n = dve.value_load(ctl[0:1, 0, ds(bb, 1)], min_val=1, max_val=NG)
                k0 = dve.value_load(ctl[0:1, 1, ds(bb, 1)], min_val=0, max_val=B * NG)
                if next_features:
                    evac_f(bb + 1, 1 - k, DC - 1)
                with dve.Fori(0, n) as g:
                    kk = k0 + g
                    for t in range(G):
                        dve.wait_ge(s_h, kk * G + t + 1)
                        dve.wait_ge(s_hfree, kk * G + t + 3)
                        chain = Chain(s_gch, kk * 2 * G + 2 * t)
                        part = partial[:, t % 2, :]
                        chain.link(dve.tensor_scalar(part, h_ring[:, t, 1, :], w_col[:, 1:2], None, ALU.mult))
                        chain.link(dve.scalar_tensor_tensor(part, h_ring[:, t, 2, :], w_col[:, 2:3], part,
                                                            ALU.mult, ALU.add))
                        dve.scalar_tensor_tensor(part, h_ring[:, t, 3, :], w_col[:, 3:4], part,
                                                 ALU.mult, ALU.add).then_inc(s_sum, 1)
                        if t == 0:
                            rows(kk + bb, kk)
                rows(k0 + n + bb, k0 + n)
                dve.wait_ge(s_row, k0 + n + bb + 2)

            def rows(copy, kk):
                dve.wait_ge(s_hfree, kk * G + G)
                dve.wait_ge(s_row, copy + 1)
                dve.tensor_copy(rho_rows[:, :], bankR[:, ds((kk + 1) % 2, 1), :].rearrange("p a f -> p (a f)"))\
                   .then_inc(s_rfree, 1)

            def gates_of_experts(bb, k):
                dve.wait_ge(s_lge, bb + 1)
                dve.tensor_reduce(psum_e[:, :], lge[:, :, :], X, ALU.add).then_inc(s_gsum, 1)
                wait_apart(dve, s_gsum, bb + 1)
                dve.reciprocal(pay[k][:, :, D + 2], psum_e[:, :]).then_inc(s_slot, 1)

            def epilogue(bb, ib, k, last):
                ep = Chain(s_ep, bb * EPI_STEPS)
                rT = bankT.rearrange("p (i t) -> p i t", i=NI)[:, :, G:G + T]

                def key_row(r):
                    return r[:, ds(bb, 1), :].broadcast_to([P, NI, T])

                ep.link(dve.tensor_tensor(z[:, :, :], rT, key_row(bias_row), ALU.add))
                ep.link(dve.tensor_reduce(mx[:, :], z[:, :, :], X, ALU.max))
                dve.tensor_tensor(z[:, :, :], z[:, :, :], mx[:, :][:, :, None].broadcast_to([P, NI, T]),
                                  ALU.subtract).then_inc(s_zs, 1)
                if not last:
                    x_lows(bb + 2)
                dve.wait_ge(s_exp, bb + 1)
                dve.tensor_reduce(nd[:, 0, :], z[:, :, :], X, ALU.add)
                ep.link(dve.tensor_tensor(pw[:, 0, :, :], z[:, :, :], key_row(cw_row), ALU.mult))
                ep.link(dve.tensor_tensor(pw[:, 1, :, :], z[:, :, :], key_row(cb_row), ALU.mult))
                dve.reciprocal(rden[:, :], nd[:, 0, :])
                ep.link(dve.tensor_reduce(nd[:, 1:3, :], pw[:, :, :, :], X, ALU.add))
                dve.tensor_tensor(ws_in[:, :, :], nd[:, 1:3, :], rden[:, None, :].broadcast_to([P, 2, NI]),
                                  ALU.mult).then_inc(s_wsin, 1)
                if not last:
                    logit_evac(bb + 2)
                gates_of_experts(bb, 1 - k)
                mean, var = one(mean_x, bb), one(var_x, bb)
                rstd, std = one(rstd_x.bitcast(fp32), bb), one(std_x, bb)
                gate, shift = ws[:, 0, :], ws[:, 1, :]
                scale, offset, tmp, sq, to_h2 = (affine[:, q, :] for q in range(5))
                dve.wait_ge(s_ws, 2 * bb + 2)
                ep.link(dve.tensor_tensor(tmp, gate, rstd, ALU.mult))
                dve.tensor_scalar(scale, tmp, 1.0, None, ALU.add)
                ep.link(dve.tensor_tensor(sq, tmp, mean, ALU.mult))
                ep.link(dve.tensor_tensor(offset, shift, sq, ALU.subtract))
                dve.sem_inc(s_affine, 1)
                dve.wait_ge(s_payfree, bb + 1)
                ep.link(dve.tensor_tensor(sq, scale, scale, ALU.mult))
                dve.tensor_tensor(pay[k][:, :, D], mean, shift, ALU.add)
                ep.link(dve.tensor_tensor(tmp, sq, var, ALU.mult))
                y, _ = rsqrt(ep, rstd_2[:, :, :], tmp[:, None, :], slice(0, 1))
                y = y.rearrange("p b i -> p (b i)")
                dve.tensor_copy(pay[k][:, :, D + 1], y)
                dve.tensor_copy(pay[k][:, :, D + 3], tokid[:, :])
                ep.link(dve.tensor_tensor(to_h2, scale, y, ALU.mult))
                ep.link(dve.tensor_tensor(to_h2, to_h2, std, ALU.mult))
                raw = lraw[k][:, :, :]
                ep.link(dve.tensor_tensor(lg[:, :, :], raw, to_h2[:, :, None].broadcast_to([P, NI, E]), ALU.mult))
                ep.link(dve.tensor_tensor(lg[:, :, :], lg[:, :, :], gb_row[:, None, :].broadcast_to([P, NI, E]), ALU.add))
                ep.link(dve.tensor_reduce(top[:, 0, :], lg[:, :, :], X, ALU.max))
                top_wide = top[:, 0, :][:, :, None].broadcast_to([P, NI, E])
                dve.tensor_tensor(lgd[:, :, :], lg[:, :, :], top_wide, ALU.subtract).then_inc(s_lgd, 1)
                ep.link(dve.tensor_tensor(eq[:, :, :], lg[:, :, :], top_wide, ALU.is_equal))
                ep.link(dve.tensor_tensor(eq[:, :, :], eq[:, :, :], erev[:, None, :].broadcast_to([P, NI, E]), ALU.mult))
                ep.link(dve.tensor_reduce(top[:, 1, :], eq[:, :, :], X, ALU.max))
                dve.wait_ge(s_ready, bb + 1)
                dve.tensor_tensor(onehot[:, :, :], eq[:, :, :], top[:, 1, :][:, :, None].broadcast_to([P, NI, E]),
                                  ALU.is_equal).then_inc(s_oh, 1)
                ep.link(dve.tensor_scalar(pos[:, 3, :], tokid[:, :], float(S), None, ALU.add))
                ep.link(dve.tensor_copy(tokid[:, :], pos[:, 3, :]))
                dve.wait_ge(s_cnt, bb + 1)
                if not last:
                    dve.wait_ge(s_lraw, bb + 3)
                    dve.tensor_copy(lraw[k][:, :, :], rawL)
                dve.tensor_copy(counts_in[:, :, :, :], cntL).then_inc(s_lread, 1)
                assert ep.n == EPI_STEPS, ep.n

            dve.sem_inc(s_row, 1)
            dve.wait_ge(s_blank, 16)
            dve.memset(lgd[:, :, :], 0.0).then_inc(s_lgd, 1)
            with dve.Fori(0, HB_ - 1) as i:
                for k in (0, 1):
                    groups(2 * i + k, k, True)
                    epilogue(2 * i + k, i, k, False)
            for k in (0, 1):
                groups(B - 2 + k, k, k == 0)
                epilogue(B - 2 + k, HB_ - 1, k, True)
            gates_of_experts(B, 1)

            fin = Chain(s_fin, 0)
            dve.wait_ge(s_ready, B + 1)
            fin.link(dve.tensor_copy(load_n[:, 0, :], run[0:1, NI, :]))
            fin.link(dve.tensor_tensor(past_tile[:, :, :], load_n[:, 0, :][:, :, None].broadcast_to([1, E, NS - 1]),
                                       tile_edge[:, :, :], ALU.is_gt))
            fin.link(dve.tensor_reduce(load_n[:, 1, :], past_tile[:, :, :], X, ALU.add))
            dve.tensor_scalar(tiles_ctl[:, :], load_n[:, 1, :], 1.0, None, ALU.add).then_inc(s_tiles, 1)
            dve.memset(PS[:, :, :], 0.0).then_inc(s_clear, 1)

            def rows_of(e):
                return xin[:, ds(e % 2, 1), :, :].rearrange("p k s d -> p (k s) d")

            def w1_low(j, k):
                dve.wait_ge(s_w1h, j + 1)
                dve.tensor_tensor(w1l[k][:, :, :], w1s[k][:, :, :], w1h[k][:, :, :].bitcast(fp32), ALU.subtract)\
                   .then_inc(s_w1l, 1)

            def w2_low(j, k):
                dve.wait_ge(s_w2h, j + 1)
                dve.tensor_tensor(w2l[k][:, :, :], w2s[k][:, :, :], w2h[k][:, :, :].bitcast(fp32), ALU.subtract)\
                   .then_inc(s_w2l, 1)

            def hidden(j, k):
                for m in range(HP):
                    part_of = (slice(None), m, slice(0, WIDE)) if m < QF else (slice(None), slice(None), slice(WIDE, CAP))
                    src, high, low = relu_out[part_of], hh[k][part_of], hl[k][part_of]
                    dve.wait_ge(s_dn, j + 1)
                    dve.wait_ge(s_hf, HP * (j + 1) + m + 1)
                    dve.tensor_copy(high, src).then_inc(s_hh, 1)
                    dve.wait_ge(s_hh, HP * j + m + 1)
                    dve.tensor_tensor(low, src, high.bitcast(fp32), ALU.subtract).then_inc(s_hl, 1)

            def x_rows(fills, e, s, b):
                dve.wait_ge(s_xin, (e + 1) * 16)
                if fills is not None:
                    dve.wait_ge(s_xf, fills)
                rows = rows_of(e)
                tile = lambda a, z: rows[:, ds(s, 1), a:z].rearrange("p s d -> p (s d)")
                dve.tensor_scalar(hx[b][:, :], tile(0, D), tile(D, D + 1), tile(D + 1, D + 2),
                                  ALU.subtract, ALU.mult).then_inc(s_hx, 1)

            def x_low(fill, e, s, bank):
                dve.wait_ge(s_xh, fill + 1)
                cols = [q[:, ds(e % 2, 1), :, ds(s * P, P)].rearrange("p k c n -> p (k c) n") for q in (xh, xl)]
                dve.tensor_tensor(cols[1], bankH[bank].rearrange("p (c n) -> p c n", c=DC), cols[0].bitcast(fp32),
                                  ALU.subtract).then_inc(s_xl, 1)

            def residual(e):
                dve.wait_ge(s_b2, (e + 1) * 16)
                dve.wait_ge(s_yfree, e + 1)
                rows = rows_of(e)
                b2e = b2wide[:, ds(e % 2, 1), :].rearrange("p k d -> p (k d)")
                for s in range(NS):
                    dve.scalar_tensor_tensor(y_out[:, s, :], b2e, rows[:, s, D + 2:D + 3], rows[:, s, 0:D],
                                             ALU.mult, ALU.add)
                dve.tensor_copy(out_idx[:, :], rows[:, :, D + 3]).then_inc(s_u, 1)

            def finish(e):
                rows = rows_of(e)
                dve.wait_ge(s_u, e + 1)
                dve.wait_ge(s_dn, (e + 1) * NU + 2)
                for s in range(NS):
                    dve.scalar_tensor_tensor(y_out[:, s, :], bankY[:, s, :], rows[:, s, D + 2:D + 3], y_out[:, s, :],
                                             ALU.mult, ALU.add).then_inc(s_yr, 1)

            def first_turn(e):
                w1_low(e * NU + 1, 1)
                hidden(e * NU, 0)
                w2_low(e * NU, 0)

            def expert(e, last):
                def pair(j, fill, p, tail):
                    w1_low(j + 1, 1)
                    if not last:
                        x_rows(fill, e + 1, p, 0)
                        x_rows(fill, e + 1, p + 2, 1)
                    hidden(j, 0)
                    if not last:
                        x_low(fill, e + 1, p, 0)
                    w2_low(j, 0)
                    if not last:
                        x_low(fill + 1, e + 1, p + 2, 1)
                    if not (last and tail):
                        w1_low(j + 2, 0)
                    hidden(j + 1, 1)
                    w2_low(j + 1, 1)

                w1_low(e * NU + 2, 0)
                hidden(e * NU + 1, 1)
                w2_low(e * NU + 1, 1)
                with dve.Fori(0, NU // 2 - 2) as p:
                    pair(e * NU + 2 * p + 2, NS + e * len(FILLS) + 2 * p, p, False)
                pair(e * NU + NU - 2, NS + (e + 1) * len(FILLS) - 2, NU // 2 - 2, True)
                residual(e)
                if not last:
                    first_turn(e + 1)
                finish(e)

            w1_low(0, 0)
            for s in range(NS + 1):
                if s < NS:
                    x_rows(s - 1 if s > 1 else None, 0, s, s % 2)
                if s > 0:
                    x_low(s - 1, 0, s - 1, (s - 1) % 2)
            first_turn(0)
            with dve.Fori(0, E - 1) as e:
                expert(e, False)
            expert(E - 1, True)

        @block.tensor
        def _(pe):
            pe.wait_ge(s_const, 17)
            pe.wait_ge(s_pre, 2)
            pe.matmul(bankT[0:T, 0:B], triu[0:T, 0:T], active[:, :], start=True, stop=True)
            pe.matmul(bankT[:, B:2 * B], ones[0:T, :], active[:, :], start=True, stop=True).then_inc(s_preA2, 1)
            def transposed(n):
                pe.wait_ge(s_xn, n + 1)
                for c in range(DC):
                    if not (isinstance(n, int) and n == 0):
                        wait_apart(pe, s_afree, n * 2 * DC - DC + c + 1)
                    for i in range(NI):
                        ins = pe.transpose(bankA[c][:, i * P:(i + 1) * P], xn[:, i, c * P:(c + 1) * P], ident[:, :])
                    ins.then_inc(s_afull, 1)

            def logit_products(n):
                if not (isinstance(n, int) and n == 0):
                    pe.wait_ge(s_lread, n)
                wait_apart(pe, s_xnhigh, n * DC + DC)
                for m, (gt, xt) in enumerate(((gwT_high, xnT_high), (gwT_low, xnT_high), (gwT_high, xnT_low))):
                    if m == 2:
                        wait_apart(pe, s_afree, n * 2 * DC + DC)
                    for c in range(DC):
                        ins = pe.matmul(bankL[0:E, :], gt[:, c, :], xt[:, c, :],
                                        start=(m == 0 and c == 0), stop=(m == 2 and c == DC - 1))
                ins.then_inc(s_lprod, 1)

            def raw_logits(n):
                wait_apart(pe, s_lrows, n + 1)
                for i in range(NI):
                    ins = pe.matmul(bankL[:, i * E:(i + 1) * E], logit_rows[:, i * P:(i + 1) * P],
                                    ident[0:E, 0:E], start=True, stop=True)
                ins.then_inc(s_lraw, 1)

            def project(n, chunks):
                wait_apart(pe, s_afree, n * 2 * DC + DC)
                for c2 in chunks:
                    for m, (wt, xt) in enumerate(((W_high, xnT_high), (W_low, xnT_high), (W_high, xnT_low))):
                        for c in range(DC):
                            ins = pe.matmul(bankA[c2], wt[:, c, c2 * P:(c2 + 1) * P], xt[:, c, :],
                                            start=(m == 0 and c == 0), stop=(m == 2 and c == DC - 1))
                    ins.then_inc(s_afull, 1)

            pe.wait_ge(s_ctx, 16)
            pe.wait_ge(s_perm, 1)
            f = 0

            def bank():
                nonlocal f
                f += 1
                if f > 2:
                    pe.wait_ge(s_preF, f - 2)
                return bankP[(f - 1) % 2]

            for n in range(B):
                bk = bank()
                for c in range(DC):
                    ins = pe.matmul(bk[:, c * T:(c + 1) * T], ctx_sb[:, n, c * P:(c + 1) * P], perm[:, n, :],
                                    start=True, stop=True)
                ins.then_inc(s_preA, 1)
            for hf in (0, 1):
                bk = bank()
                for n in range(HB_):
                    ins = pe.matmul(bk[:, n * T:(n + 1) * T], maskw[:, hf * HB_ + n, :], perm[:, hf * HB_ + n, :],
                                    start=True, stop=True)
                ins.then_inc(s_preA, 1)

            def keys(c, hf):
                return ctxT[:, c, hf * HB_:(hf + 1) * HB_, :].rearrange("p b t -> p (b t)")

            pe.wait_ge(s_preF, B)
            pe.wait_ge(s_Ws, 16)
            for c2 in range(DC):
                for hf in (0, 1):
                    bk = bank()
                    for c in range(DC):
                        ins = pe.matmul(bk[:, 0:HB_ * T], Ws_sb[:, c, c2 * P:(c2 + 1) * P], keys(c, hf),
                                        start=(c == 0), stop=(c == DC - 1))
                    ins.then_inc(s_preA, 1)
            assert f == PRE_FILLS
            transposed(0)
            pe.wait_ge(s_Wsplit, 2)
            project(0, range(DC))
            pe.wait_ge(s_ldw, 9 * 16)
            pe.wait_ge(s_preF, PRE_FILLS)
            for c in range(DC):
                ins = pe.transpose(bankP[1][:, c * E:(c + 1) * E], gw_rows[:, c * P:(c + 1) * P], ident[0:E, 0:E])
            ins.then_inc(s_gw, 1)
            pe.wait_ge(s_gwr, 1)
            logit_products(0)
            raw_logits(0)
            transposed(1)
            logit_products(1)
            project(1, range(DC - 1))
            raw_logits(1)
            pe.wait_ge(s_wide, 1)
            late = 0
            for m in (0, 1):
                for hf in (0, 1):
                    late += 1
                    if late > 2:
                        pe.wait_ge(s_lateF, late - 2)
                    for c in range(DC):
                        ins = pe.matmul(bankP[late % 2][:, 0:HB_ * T], wc_wide[:, m, c, :], keys(c, hf),
                                        start=(c == 0), stop=(c == DC - 1))
                    ins.then_inc(s_preA, 1)
            pe.wait_ge(s_lateF, late - 1)
            pe.transpose(bankP[(late + 1) % 2][:, 0:E * NF], b1rows[:, :], ident[:, :]).then_inc(s_preA, 1)
            pe.wait_ge(s_lateF, late + 1)
            pe.wait_ge(s_ctl, 1)

            def tokens_first(copy, g):
                wait_apart(pe, s_rfree, copy + 2)
                for i in range(NI):
                    ins = pe.matmul(bankT[:, ds(g * G + i * P, G)], rho_rows[:, i * P:(i + 1) * P],
                                    ident[0:G, 0:G], start=True, stop=True)
                ins.then_inc(s_row, 1)

            def batch(bb, k, last, next_features=True):
                if next_features:
                    project(bb + 1, [DC - 1])
                n = pe.value_load(ctl[0:1, 0, ds(bb, 1)], min_val=1, max_val=NG)
                k0 = pe.value_load(ctl[0:1, 1, ds(bb, 1)], min_val=0, max_val=B * NG)
                with pe.Fori(0, n) as g:
                    kk = k0 + g
                    pe.wait_ge(s_rfree, kk + bb + 1)
                    bk = bankR[:, ds(kk % 2, 1), :].rearrange("p a f -> p (a f)")
                    for t in range(G):
                        wait_apart(pe, s_h, kk * G + t + 1)
                        pe.matmul(bk, wsel[:, t, :], h_ring[:, t, 0, :], start=(t == 0), stop=False)
                        wait_apart(pe, s_sum, kk * G + t + 1)
                        pe.matmul(bk, onesel[:, t, :], partial[:, t % 2, :], start=False,
                                  stop=(t == G - 1)).then_inc(s_hfree, 1)
                        if t == 0:
                            tokens_first(kk + bb, g)
                tokens_first(k0 + n + bb, n)
                if not last:
                    transposed(bb + 2)
                    logit_products(bb + 2)
                    project(bb + 2, range(DC - 1))
                    raw_logits(bb + 2)
                pe.wait_ge(s_oh, bb + 1)
                pe.wait_ge(s_lread, bb + 2)
                oh = onehot[:, :, :].rearrange("p i e -> p (i e)")
                pe.matmul(bankL[:, NI * E:2 * NI * E], triu[:, :], oh, start=True, stop=True)
                pe.matmul(bankL[:, 2 * NI * E:3 * NI * E], ones[:, :], oh, start=True, stop=True).then_inc(s_cnt, 1)

            with pe.Fori(0, HB_ - 1) as i:
                for k in (0, 1):
                    batch(2 * i + k, k, False)
            for k in (0, 1):
                batch(B - 2 + k, k, True, next_features=(k == 0))

            pe.wait_ge(s_tiles, 1)
            pe.wait_ge(s_clear, 1)

            def by_tiles(n, emit):
                with pe.If(n < NW):
                    emit(NW - 1)
                with pe.Else():
                    with pe.If(n < NS):
                        emit(NW)
                    with pe.Else():
                        emit(NS)

            def fill(n, b, j=None):
                pe.wait_ge(s_hx, n + 1)
                if j is None:
                    if n > 1:
                        pe.wait_ge(s_xl, n - 1)
                else:
                    pe.wait_ge(s_hf, HP * (j + 1) + b + 1)
                for c in range(DC):
                    ins = pe.transpose(bankH[b][:, c * P:(c + 1) * P], hx[b][:, c * P:(c + 1) * P], ident[:, :])
                ins.then_inc(s_xf, 1)

            def up(e, j, k, n, fills):
                pe.wait_ge(s_w1l, j + 1)
                pe.wait_ge(s_xl, fills)
                pe.wait_ge(s_hf, HP * (j + 1))

                def product(dst, f, a, z):
                    for c in range(DC):
                        for m, (wt, xt) in enumerate(((w1h, xh), (w1h, xl), (w1l, xh))):
                            ins = pe.matmul(dst, wt[k][:, c, f * P:(f + 1) * P],
                                            xt[:, ds(e % 2, 1), c, a:z].rearrange("p k n -> p (k n)"),
                                            start=(c == 0 and m == 0), stop=(c == DC - 1 and m == 2))
                    return ins

                def emit(tiles):
                    wide = min(tiles, NW) * P
                    for f in range(QF):
                        product(bankH[f][:, 0:wide], f, 0, wide).then_inc(s_up, 1)
                    if tiles > NW:
                        for f in range(QF):
                            ins = product(bankH4[:, f * P:(f + 1) * P], f, WIDE, CAP)
                        ins.then_inc(s_up, 1)
                    else:
                        pe.matmul(bankH4[:, 0:P], w1h[k][:, 0, 0:P],
                                  xh[:, ds(e % 2, 1), 0, WIDE:CAP].rearrange("p k n -> p (k n)"),
                                  start=True, stop=True).then_inc(s_up, 1)

                by_tiles(n, emit)

            def down(j, k, n, first=False, between=None):
                pe.wait_ge(s_w2l, j + 1)
                pe.wait_ge(s_hl, HP * (j + 2))

                def emit(tiles):
                    for f in range(QF):
                        if f == QF - 1 and between is not None:
                            between()
                        for s in range(tiles):
                            for m, (ht, wt) in enumerate(((hh, w2h), (hh, w2l), (hl, w2h))):
                                ins = pe.matmul(bankY[:, s, :], ht[k][:, f, s * P:(s + 1) * P], wt[k][:, f, :],
                                                start=(first and f == 0 and m == 0), stop=True,
                                                skip_group_check=True)
                    ins.then_inc(s_dn, 1)

                by_tiles(n, emit)

            def expert(e, last):
                n = pe.value_load(tiles_ctl[0:1, ds(e, 1)], min_val=1, max_val=NS)
                base = NS + e * len(FILLS)
                up(e, e * NU + 1, 1, n, base)
                pe.wait_ge(s_yr, e * NS + 1)
                down(e * NU, 0, n, first=True)

                def pair(j, b):
                    up(e, j, 0, n, b)
                    if not last:
                        fill(b, 0, j)
                    down(j - 1, 1, n, between=None if last else lambda: fill(b + 1, 1, j))
                    up(e, j + 1, 1, n, base if last else b + 2)
                    down(j, 0, n)

                with pe.Fori(0, NU // 2 - 1) as p:
                    pair(e * NU + 2 * p + 2, base if last else base + 2 * p)
                if not last:
                    n_next = pe.value_load(tiles_ctl[0:1, ds(e + 1, 1)], min_val=1, max_val=NS)
                    up(e + 1, (e + 1) * NU, 0, n_next, base + len(FILLS))
                down(e * NU + NU - 1, 1, n)

            for m in range(NS):
                fill(m, m % 2)
            n_first = pe.value_load(tiles_ctl[0:1, 0:1], min_val=1, max_val=NS)
            up(0, 0, 0, n_first, NS)
            with pe.Fori(0, E - 1) as e:
                expert(e, False)
            expert(E - 1, True)


_INS = ['x', 'ctx_1024', 'mask_BxS2_ik0', 'L0_xattn_Ws', 'L0_xattn_W', 'L0_xattn_w', 'L0_xattn_b', 'L0_xattn_Wcw',
        'L0_xattn_bcw', 'L0_xattn_Wcb', 'L0_xattn_bcb', 'L0_ffn_gate_w', 'L0_ffn_gate_b', 'L0_ffn_w1', 'L0_ffn_b1',
        'L0_ffn_w2', 'L0_ffn_b2']


def kernel(**inputs):
    import numpy as _np
    import concourse.bacc as _bacc
    from concourse import mybir as _mybir
    from concourse.bass_utils import run_bass_kernel_spmd as _run

    nc = _bacc.Bacc("TRN2", target_bir_lowering=False, num_devices=1)
    arrays, args = {}, []
    for name in _INS:
        a = _np.ascontiguousarray(inputs[name])
        arrays[f"in_{name}_dram"] = a
        args.append(nc.dram_tensor(f"in_{name}_dram", a.shape, _mybir.dt.from_np(a.dtype), kind="ExternalInput").ap())
    shape = inputs['x'].shape
    out = nc.dram_tensor("out_0_dram", shape, _mybir.dt.float32, kind="ExternalOutput").ap()
    xattn_moe_kernel(nc, *args, out)
    r = _run(nc, [arrays], core_ids=[0])
    return r.results[0]["out_0_dram"]
```
